# Optimizing a Trainium2 kernel written in Bass

```python
import numpy as np
import jax
import jax.numpy as jnp

def _softmax(x, axis=-1):
    return jax.nn.softmax(x, axis=axis)

def _gelu(x):
    return jax.nn.gelu(x, approximate=True)

def _silu(x):
    return jax.nn.silu(x)

def _sigmoid(x):
    return jax.nn.sigmoid(x)

def _layernorm(x, axis=-1, eps=1e-05):
    m = jnp.mean(x, axis=axis, keepdims=True)
    v = jnp.var(x, axis=axis, keepdims=True)
    return (x - m) / jnp.sqrt(v + eps)

def _scatter_add(tgt, idx, src, axis=0):
    return tgt.at[idx].add(src)

def _segment_sum(src, seg, n):
    return jax.ops.segment_sum(src, seg, n)
kernel_name = 'mk_gnn_preln_d2_gnn_r64_27f813'

def setup_inputs(seed: int=0):
    np.random.seed(seed)
    _w = jnp.asarray

    def _rec_inputs():
        import jax
        import jax.numpy as jnp
        _gk = jax.random.key(seed)
        x = -0.0003929 + 0.9999 * jax.random.normal(jax.random.fold_in(_gk, 1), (256, 1024), jnp.float32)
        _s = jax.random.randint(jax.random.fold_in(_gk, 2), (4096,), 0, 256, jnp.int32)
        _d = jax.random.randint(jax.random.fold_in(_gk, 3), (4096,), 0, 256, jnp.int32)
        _loop = jnp.arange(256, dtype=jnp.int32)
        src = jnp.concatenate([_s, _d, _loop])
        dst = jnp.concatenate([_d, _s, _loop])
        _o = jnp.argsort(dst, stable=True)
        src = src[_o]
        dst = dst[_o]
        edge_weight = -0.000130211 + 0.031236 * jax.random.normal(jax.random.fold_in(_gk, 13), (8448,), jnp.float32)
        return (x, src, dst, edge_weight)
    x, src, dst, edge_weight = _rec_inputs()

    def _L0_gnn_setup():
        import jax, jax.numpy as jnp
        import numpy as np
        NH, NO = (64, 192)
        N = NH + NO
        E_HH, E_OO, E_HO = (128, 640, 256)
        E = E_HH + E_OO + E_HO
        D = 1024
        key = jax.random.key(seed)
        ks = jax.random.split(key, 12)
        w = lambda k, s: jax.random.normal(k, s, jnp.float32) * 0.02
        return {'n_f': jax.random.normal(ks[0], (N, D), jnp.float32), 'W_hh': w(ks[1], (2 * D, D)), 'b_hh': jnp.zeros((D,), jnp.float32), 'W_oo': w(ks[2], (2 * D, D)), 'b_oo': jnp.zeros((D,), jnp.float32), 'W_ho': w(ks[3], (2 * D, D)), 'b_ho': jnp.zeros((D,), jnp.float32), 'W_a': w(ks[4], (D, 1)), 'b_a': jnp.zeros((1,), jnp.float32), 'W_hn': w(ks[5], (2 * D, D)), 'b_hn': jnp.zeros((D,), jnp.float32), 'W_on': w(ks[6], (2 * D, D)), 'b_on': jnp.zeros((D,), jnp.float32), 'edge_src': jax.random.randint(ks[7], (E,), 0, N, jnp.int32), 'edge_dst': jax.random.randint(ks[8], (E,), 0, N, jnp.int32)}
    _L0_gnn_all = _L0_gnn_setup()
    _L0_gnn_in = {k: v for k, v in _L0_gnn_all.items() if k in ('W_hh', 'b_hh', 'W_oo', 'b_oo', 'W_ho', 'b_ho', 'W_a', 'b_a', 'W_hn', 'b_hn', 'W_on', 'b_on')}
    del _L0_gnn_all

    def _L1_gnn_setup():
        import jax, jax.numpy as jnp
        import numpy as np
        INDIM = 1024
        OUTDIM = 1024
        NNZ = 1024
        N = 50000
        key = jax.random.key(seed)
        k1, k2, k3, k4, k5 = jax.random.split(key, 5)
        x = jax.random.normal(k1, (N, INDIM), dtype=jnp.float32)
        stdv = np.sqrt(6.0 / (INDIM + OUTDIM))
        nnz_weight = jax.random.uniform(k2, (NNZ,), dtype=jnp.float32, minval=-stdv, maxval=stdv)
        bias = jax.random.normal(k3, (OUTDIM,), dtype=jnp.float32) * 0.02
        row = jax.random.randint(k4, (NNZ,), 0, OUTDIM, dtype=jnp.int64)
        col = jax.random.randint(k5, (NNZ,), 0, INDIM, dtype=jnp.int64)
        edge_index = jnp.stack([row, col])
        return {'x': x, 'nnz_weight': nnz_weight, 'bias': bias, 'edge_index': edge_index}
    _L1_gnn_all = _L1_gnn_setup()
    _L1_gnn_in = {k: v for k, v in _L1_gnn_all.items() if k in ('bias',)}
    del _L1_gnn_all
    return {'x': x, 'src': src, 'dst': dst, 'edge_weight': edge_weight, 'L0_gnn_W_hh': _L0_gnn_in['W_hh'], 'L0_gnn_b_hh': _L0_gnn_in['b_hh'], 'L0_gnn_W_oo': _L0_gnn_in['W_oo'], 'L0_gnn_b_oo': _L0_gnn_in['b_oo'], 'L0_gnn_W_ho': _L0_gnn_in['W_ho'], 'L0_gnn_b_ho': _L0_gnn_in['b_ho'], 'L0_gnn_W_a': _L0_gnn_in['W_a'], 'L0_gnn_b_a': _L0_gnn_in['b_a'], 'L0_gnn_W_hn': _L0_gnn_in['W_hn'], 'L0_gnn_b_hn': _L0_gnn_in['b_hn'], 'L0_gnn_W_on': _L0_gnn_in['W_on'], 'L0_gnn_b_on': _L0_gnn_in['b_on'], 'L1_gnn_bias': _L1_gnn_in['bias']}

def reference(x, src, dst, edge_weight, L0_gnn_W_hh, L0_gnn_b_hh, L0_gnn_W_oo, L0_gnn_b_oo, L0_gnn_W_ho, L0_gnn_b_ho, L0_gnn_W_a, L0_gnn_b_a, L0_gnn_W_hn, L0_gnn_b_hn, L0_gnn_W_on, L0_gnn_b_on, L1_gnn_bias):
    import jax
    import jax.numpy as jnp

    def _L0_gnn_ref(n_f, W_hh, b_hh, W_oo, b_oo, W_ho, b_ho, W_a, b_a, W_hn, b_hn, W_on, b_on, edge_src, edge_dst):
        import jax, jax.numpy as jnp
        import numpy as np
        NH, NO = (64, 192)
        N = NH + NO
        E_HH, E_OO, E_HO = (128, 640, 256)
        E = E_HH + E_OO + E_HO
        D = 1024
        feat = jnp.concatenate([n_f[edge_src], n_f[edge_dst]], axis=1)
        e_hh = jax.nn.relu(feat[:E_HH] @ W_hh + b_hh)
        e_oo = jax.nn.relu(feat[E_HH:E_HH + E_OO] @ W_oo + b_oo)
        e_ho = jax.nn.relu(feat[E_HH + E_OO:] @ W_ho + b_ho)
        e_f = jnp.concatenate([e_hh, e_oo, e_ho], axis=0)
        logit = (e_f @ W_a + b_a)[:, 0]
        m = jax.lax.stop_gradient(jax.ops.segment_max(logit, edge_dst, num_segments=N))
        ex = jnp.exp(logit - m[edge_dst])
        den = jax.ops.segment_sum(ex, edge_dst, num_segments=N)
        alpha = ex / den[edge_dst]
        z_f = jax.ops.segment_sum(alpha[:, None] * n_f[edge_src], edge_dst, num_segments=N)
        nf2 = jnp.concatenate([n_f, z_f], axis=1)
        h_new = jax.nn.relu(nf2[:NH] @ W_hn + b_hn)
        o_new = jax.nn.relu(nf2[NH:] @ W_on + b_on)
        return jnp.concatenate([h_new, o_new], axis=0)

    def _L1_gnn_ref(x, nnz_weight, bias, edge_index):
        import jax, jax.numpy as jnp
        import numpy as np
        INDIM = 1024
        OUTDIM = 1024
        NNZ = 1024
        N = 50000
        row, col = (edge_index[0], edge_index[1])
        W = jnp.zeros((OUTDIM, INDIM), dtype=nnz_weight.dtype).at[row, col].add(nnz_weight)
        return x @ W.T + bias
    edge_index = jnp.stack([src, dst])
    h = jnp.maximum(_layernorm(x, axis=-1), 0.0)
    x = x + _L0_gnn_ref(h, L0_gnn_W_hh, L0_gnn_b_hh, L0_gnn_W_oo, L0_gnn_b_oo, L0_gnn_W_ho, L0_gnn_b_ho, L0_gnn_W_a, L0_gnn_b_a, L0_gnn_W_hn, L0_gnn_b_hn, L0_gnn_W_on, L0_gnn_b_on, src, dst)
    h = jnp.maximum(_layernorm(x, axis=-1), 0.0)
    x = x + _L1_gnn_ref(h, edge_weight, L1_gnn_bias, edge_index)
    return x

_drawn_inputs = setup_inputs


def setup_inputs(seed=0):
    import zlib

    import numpy as np

    out = dict(_drawn_inputs(seed))
    spreads = {'L0_gnn_b_hh': (0.0, 2.0),
     'L0_gnn_b_oo': (0.0, 2.0),
     'L0_gnn_b_ho': (0.0, 0.8),
     'L0_gnn_b_hn': (0.0, 0.1),
     'L0_gnn_b_on': (0.0, 0.1)}
    factors = {'L0_gnn_W_hh': 21.838,
     'L0_gnn_W_oo': 8.0,
     'L0_gnn_W_ho': 8.0,
     'L0_gnn_W_a': 8.0,
     'L1_gnn_bias': 2.968}
    for name, (base, spread) in spreads.items():
        noise = np.random.default_rng([zlib.crc32(name.encode()), seed]).standard_normal(out[name].shape)
        drawn = base * np.exp(spread * noise) if base else spread * noise
        out[name] = jnp.asarray(drawn.astype(out[name].dtype))
    for name, factor in factors.items():
        out[name] = (out[name] * factor).astype(out[name].dtype)
    return out
```

```python
import concourse.bass as bass
from concourse import mybir
from contextlib import ExitStack

P = 128
N = 256
NT = N // P
D = 1024
KC = D // P
HALF = 512
E = 8448
ET = E // P
NH = 64
GT = 6
OO_TILES = 5
HO0 = 1 + OO_TILES
HO_TILES = ET - HO0
PAIRS = HO_TILES // (2 * GT)
UNITS = 10
WSLOTS = 4
RING = 3
NEG = -3.0e38
EPS = 1e-5
CAST = 1056


def gnn_block(nc, x, edge_ids, dst_row, edge_w, weights, bias_rows, b_oo, w_a, b_a, l1_bias, out):
    f32, f32r, bf16, i32 = mybir.dt.float32, mybir.dt.float32r, mybir.dt.bfloat16, mybir.dt.int32
    ALU = mybir.AluOpType
    ACT = mybir.ActivationFunctionType
    AX = mybir.AxisListType

    h_rows = nc.dram_tensor("h_rows", (N, D), f32, kind="Internal").ap()
    p_ho = nc.dram_tensor("p_ho", (N, D), f32, kind="Internal").ap()
    q_ho = nc.dram_tensor("q_ho", (N, D), f32, kind="Internal").ap()
    p_oo = nc.dram_tensor("p_oo", (N, D), f32, kind="Internal").ap()
    q_oo = nc.dram_tensor("q_oo", (N, D), f32, kind="Internal").ap()
    by_tile = lambda t: t.rearrange("(a p) d -> p a d", p=P)

    ctx = ExitStack()
    with ctx:
        sb = lambda name, shape, dt: ctx.enter_context(nc.sbuf_tensor(name, shape, dt))
        pb = lambda name, shape, dt: ctx.enter_context(nc.psum_tensor(name, shape, dt))
        sem = lambda name: ctx.enter_context(nc.semaphore(name))

        xs = sb("xs", [P, NT, D], f32)
        h = sb("h", [P, NT, D], f32)
        hT = sb("hT", [P, KC, N], f32)
        hsT = sb("hsT", [P, 2, KC, P], f32)
        W = sb("W", [P, WSLOTS, 2, D], f32)
        T = sb("T", [P, 4, NT, D], f32)
        G = sb("G", [P, GT, D], f32)
        wa = sb("wa", [P, D], f32)
        boo = sb("boo", [P, D], f32)
        lb = sb("lb", [P, D], f32)
        brow = sb("brow", [4, D], f32)
        sel = sb("sel", [4, 4, P], f32)
        ids = sb("ids", [P, ET, 2], i32)
        idf = sb("idf", [P, ET, 2], f32)
        ew = sb("ew", [P, ET], f32)
        ewh = sb("ewh", [P, ET], f32r)
        ewl = sb("ewl", [P, ET], f32r)
        stage_p = sb("stage_p", [P, 2 * GT], i32)
        stage_q = sb("stage_q", [P, 2 * GT], i32)
        stage_h = sb("stage_h", [P, 2], i32)
        dstb = sb("dstb", [P, E], bf16)
        eqT = sb("eqT", [P, 2, NT, GT * P], bf16)
        negm = sb("negm", [P, NT, GT * P], bf16)
        masked = sb("masked", [P, NT, GT * P], bf16)
        ident = sb("ident", [P, P], f32)
        iota = sb("iota", [P, N], f32)
        pid = sb("pid", [P, NT], f32)
        zero = sb("zero", [P, HALF], bf16)
        bar = sb("bar", [P, 1], f32)
        st = sb("st", [P, NT, 2, 6], f32)
        mv = sb("mv", [P, NT, 2], f32)
        sd = sb("sd", [P, NT], f32)
        rs = sb("rs", [P, NT], f32)
        nb = sb("nb", [P, NT], f32)
        epst = sb("epst", [P, 1], f32)
        lg = sb("lg", [P, 2, GT], f32)
        lg0 = sb("lg0", [P, 1], f32)
        mx = sb("mx", [P, 2, NT], f32)
        mres = sb("mres", [P, 2, NT], f32)
        msp = sb("msp", [P, NT, 3], bf16)
        mg = sb("mg", [P, GT], f32)
        ed = sb("ed", [P, GT + NT], f32)
        ex = sb("ex", [P, GT + NT], f32)
        exh = sb("exh", [P, GT], f32r)
        exl = sb("exl", [P, GT], f32r)
        ohd = sb("ohd", [P, RING, N], f32r)
        R = sb("R", [P, RING, 4, N], f32r)
        A = sb("A", [P, NT, N], f32)
        AT = sb("AT", [P, NT, N], f32)
        den = sb("den", [P, NT], f32)
        Wd = sb("Wd", [P, NT, N], f32)
        h2 = sb("h2", [P, NT, N], f32)
        h2T = sb("h2T", [P, NT, N], f32)

        psG = pb("psG", [P, 4, HALF], f32)
        psB = pb("psB", [P, 2, HALF], f32)
        psA = pb("psA", [P, NT, N], f32)
        psW = pb("psW", [P, NT, N], f32)
        psM = psB[:, 0, GT // 2 * P:GT // 2 * P + 3 * GT]
        rowsB = psB[:, :, 0:GT // 2 * P]

        s_x, s_ids, s_ew, s_wa, s_small, s_dstb = map(sem, ("x_in", "ids_in", "ew_in", "wa_in", "small_in", "dstb_in"))
        s_w = [sem(f"w_in{i}") for i in range(WSLOTS)]
        s_wfree = sem("w_used")
        s_const, s_pool = sem("const_made"), sem("pool_step")
        s_hst, s_hg = sem("h_stored"), [sem("hsrc_in"), sem("hdst_in")]
        s_tab = [sem("p_ho_stored"), sem("q_ho_stored"), sem("p_oo_stored"), sem("q_oo_stored")]
        s_gp = [sem(f"p_rows{i}") for i in range(GT)]
        s_gq = [sem(f"q_rows{i}") for i in range(GT)]
        s_claim = sem("slot_claimed")
        s_used = sem("rows_used")
        s_v, s_a, s_t = sem("vector_step"), sem("scalar_step"), sem("tensor_step")
        s_h, s_hT, s_hTc = sem("h_made"), sem("hT_made"), sem("hT_copied")
        s_hsT, s_hsTc = sem("hsT_made"), sem("hsT_copied")
        s_evac = sem("unit_copied")
        s_hTd, s_ewh = sem("hT_copied_too"), sem("weights_high")
        s_hh = sem("hh_logit")
        s_lg, s_bc, s_m, s_mg = sem("logits_ready"), sem("logit_rows"), sem("max_ready"), sem("edge_max")
        s_ed, s_ex = sem("exp_in"), sem("exp_out")
        s_oh, s_ohu = sem("onehot_ready"), sem("onehot_used")
        s_acc = sem("group_added")
        s_boo = sem("b_oo_added")
        s_AT, s_ATc, s_up = sem("AT_made"), sem("AT_copied"), sem("update_made")
        s_Wd, s_st2, s_sd2, s_nb2, s_h2 = sem("Wd_copied"), sem("var2"), sem("std2"), sem("norm2"), sem("h2_made")
        s_h2T, s_h2Tc, s_y, s_o, s_out = sem("h2T_made"), sem("h2T_copied"), sem("y_made"), sem("out_ready"), sem("out_stored")
        s_var, s_sd, s_nb = sem("var1"), sem("std1"), sem("norm1")
        s_ind = sem("onehotT_ready")
        s_rowsok = sem("rows_claimed")

        block = ctx.enter_context(nc.Block())

        @block.sync
        def _(sp):
            for t in range(NT):
                sp.dma_start(xs[:, t, :], by_tile(x)[:, t, :]).then_inc(s_x, 16)
            sp.dma_start(ids[:, :, :], edge_ids).then_inc(s_ids, 16)

            def load(u, s):
                row = (u * KC + 2 * s) * P
                sp.dma_start(W[:, s, :, :],
                             weights[bass.ds(row, 2 * P), :].rearrange("(a p) d -> p a d", p=P)).then_inc(s_w[s], 16)

            for s in range(WSLOTS):
                load(0, s)
            sp.dma_start(ew[:, :], edge_w).then_inc(s_ew, 16)
            sp.dma_start(wa[:, :], w_a.broadcast_to((P, D))).then_inc(s_wa, 16)
            sp.dma_start(boo[:, :], b_oo.broadcast_to((P, D))).then_inc(s_small, 16)
            sp.dma_start(lb[:, :], l1_bias.broadcast_to((P, D))).then_inc(s_small, 16)
            sp.dma_start(brow[:, :], bias_rows).then_inc(s_small, 16)
            sp.dma_start(bar[:, :], b_a.broadcast_to((P, 1))).then_inc(s_small, 16)
            with sp.Fori(1, UNITS) as u:
                for s in range(WSLOTS):
                    sp.wait_ge(s_wfree, u * WSLOTS + s + 1 - WSLOTS)
                    load(u, s)
            for t in range(NT):
                sp.wait_ge(s_o, t + 1)
                sp.dma_start(by_tile(out)[:, t, :], xs[:, t, :]).then_inc(s_out, 16)
            sp.wait_ge(s_out, 16 * NT)

        @block.gpsimd
        def _(pool):
            nc.gpsimd.memset(ident[:, :], 0.0).then_inc(s_pool, 1)
            nc.gpsimd.memset(sel[:, :, :], 0.0).then_inc(s_pool, 1)
            nc.gpsimd.memset(zero[:, :], 0.0)
            nc.gpsimd.memset(epst[:, :], EPS)
            nc.gpsimd.memset(A[:, :, :], 0.0)
            nc.gpsimd.memset(mx[:, 1, :], NEG)
            nc.gpsimd.iota(iota[:, :], pattern=[[1, N]], base=0, channel_multiplier=0,
                           allow_small_or_imprecise_dtypes=True)
            nc.gpsimd.iota(pid[:, :], pattern=[[P, NT]], base=0, channel_multiplier=1,
                           allow_small_or_imprecise_dtypes=True)
            pool.wait_ge(s_pool, 2)
            nc.gpsimd.affine_select(out=ident[:, :], in_=ident[:, :], compare_op=ALU.not_equal, fill=1.0, base=0,
                                    pattern=[[-1, P]], channel_multiplier=1)
            nc.gpsimd.affine_select(out=sel[:, :, :], in_=sel[:, :, :], compare_op=ALU.not_equal, fill=1.0, base=0,
                                    pattern=[[-1, 4], [0, P]], channel_multiplier=1).then_inc(s_const, 1)
            pool.wait_ge(s_ids, 16)
            nc.gpsimd.tensor_copy(stage_h[:, :], ids[:, 0, :])
            nc.gpsimd.tensor_copy(stage_p[:, :], ids[:, HO0:HO0 + 2 * GT, 0])
            nc.gpsimd.tensor_copy(stage_q[:, :], ids[:, HO0:HO0 + 2 * GT, 1])
            nc.gpsimd.tensor_copy(idf[:, :, :], ids[:, :, :]).then_inc(s_pool, 1)
            pool.wait_ge(s_pool, 3)
            pool.wait_ge(s_hst, 16)
            for c in range(2):
                nc.gpsimd.indirect_dma_start(out=G[:, c, :], out_offset=None, in_=h_rows,
                                             in_offset=bass.IndirectOffsetOnAxis(ap=stage_h[:, c:c + 1], axis=0)
                                             ).then_inc(s_hg[c], 16)
            for c in range(E // CAST):
                pool.dma_start(dstb[:, c * CAST:(c + 1) * CAST],
                               dst_row[:, c * CAST:(c + 1) * CAST].broadcast_to((P, CAST))).then_inc(s_dstb, 16)

            def p_rows(n, slot, table, j):
                nc.gpsimd.indirect_dma_start(out=G[:, slot, :], out_offset=None, in_=table,
                                             in_offset=bass.IndirectOffsetOnAxis(ap=stage_p[:, j:j + 1], axis=0)
                                             ).then_inc(s_gp[slot], 16)

            def q_rows(lap, slot, table, j):
                pool.wait_ge(s_gp[slot], 16 * (lap + 1))
                pool.sem_inc(s_claim, 1)
                nc.gpsimd.indirect_dma_start(out=G[:, slot, :], out_offset=None, in_=table,
                                             in_offset=bass.IndirectOffsetOnAxis(ap=stage_q[:, j:j + 1], axis=0),
                                             compute_op=ALU.add).then_inc(s_gq[slot], 16)

            LAG = 3

            def stage(dst_tile, i, col, count, tile0):
                nc.gpsimd.tensor_copy(dst_tile[:, 0:count], ids[:, bass.ds(tile0, count), col])

            def pair(i, first, last):
                n0 = 2 * GT * i
                for j in range(2 * GT):
                    slot = j % GT
                    if not (first and j < GT):
                        pool.wait_ge(s_used, n0 + j + 1 - GT)
                        pool.sem_inc(s_claim, 1)
                    if first and j == 0:
                        pool.wait_ge(s_tab[0], 16)
                        pool.wait_ge(s_hsT, 4)
                    p_rows(n0 + j, slot, p_ho, j)
                    if j == LAG - 1 and not first:
                        for k in range(GT):
                            pool.wait_ge(s_gq[k], 16 * 2 * i)
                        pool.sem_inc(s_claim, 1)
                        nc.gpsimd.tensor_copy(stage_q[:, :], ids[:, bass.ds(HO0 + n0, 2 * GT), 1]
                                              ).then_inc(s_pool, 1)
                        pool.wait_ge(s_pool, 3 + 2 * i)
                        pool.sem_inc(s_claim, 1)
                    if j >= LAG:
                        if first and j == LAG:
                            pool.wait_ge(s_tab[1], 16)
                        k = j - LAG
                        q_rows(2 * i + k // GT, k % GT, q_ho, k)
                for k in range(2 * GT - LAG, 2 * GT):
                    q_rows(2 * i + k // GT, k % GT, q_ho, k)
                if not last:
                    nc.gpsimd.tensor_copy(stage_p[:, :], ids[:, bass.ds(HO0 + n0 + 2 * GT, 2 * GT), 0]
                                          ).then_inc(s_pool, 1)
                    pool.wait_ge(s_pool, 4 + 2 * i)
                    pool.sem_inc(s_claim, 1)

            pair(0, True, False)
            with pool.Fori(1, PAIRS - 1) as i:
                pair(i, False, False)
            pair(PAIRS - 1, False, True)
            nc.gpsimd.tensor_copy(stage_p[:, 0:OO_TILES], ids[:, 1:HO0, 0]).then_inc(s_pool, 1)
            for k in range(GT):
                pool.wait_ge(s_gq[k], 16 * 2 * PAIRS)
            nc.gpsimd.tensor_copy(stage_q[:, 0:OO_TILES], ids[:, 1:HO0, 1]).then_inc(s_pool, 1)
            pool.wait_ge(s_pool, 3 + 2 * (PAIRS - 1) + 2)
            pool.wait_ge(s_tab[2], 16)
            pool.wait_ge(s_tab[3], 16)
            for j in range(OO_TILES):
                pool.wait_ge(s_used, HO_TILES + j + 1 - GT)
                p_rows(HO_TILES + j, j, p_oo, j)
            for j in range(OO_TILES):
                q_rows(2 * PAIRS, j, q_oo, j)

        @block.scalar
        def _(act):
            steps = [0]

            def done(ins):
                steps[0] += 1
                ins.then_inc(s_a, 1)
                act.wait_ge(s_a, steps[0])

            act.wait_ge(s_var, NT)
            act.wait_ge(s_const, 1)
            nc.scalar.activation(sd[:, :], mv[:, :, 1], ACT.Sqrt, bias=epst[:, 0:1]).then_inc(s_sd, 1)
            for t in range(NT):
                act.wait_ge(s_nb, 1)
                nc.scalar.activation(h[:, t, :], xs[:, t, :], ACT.Relu, bias=nb[:, t:t + 1],
                                     scale=rs[:, t:t + 1]).then_inc(s_h, 1)
            act.wait_ge(s_h, NT)
            act.dma_start(by_tile(h_rows), h[:, :, :]).then_inc(s_hst, 16)
            for b in range(2):
                act.wait_ge(s_hT, b + 1)
                nc.scalar.copy(hT[:, 2 * b:2 * b + 2, :], psG[:, b, :].rearrange("p (k n) -> p k n", n=N)
                               ).then_inc(s_hTc, 1)
            act.wait_ge(s_ew, 16)
            nc.scalar.copy(ewh[:, :], ew[:, :]).then_inc(s_ewh, 1)

            def evac(u, dst, banks):
                act.wait_ge(s_wfree, WSLOTS * (u + 1))
                for b in range(banks):
                    nc.scalar.copy(dst(b), psG[:, b, :]).then_inc(s_evac, 1)

            def table(i):
                return lambda b: T[:, i, b // 2, bass.ds(b % 2 * HALF, HALF)]

            evac(0, table(0), 4)
            act.wait_ge(s_evac, 4)
            act.dma_start(by_tile(p_ho), T[:, 0, :, :]).then_inc(s_tab[0], 16)
            for r in range(4):
                act.wait_ge(s_hsT, r + 1)
                nc.scalar.copy(hsT[:, r // 2, 4 * (r % 2):4 * (r % 2) + 4, :],
                               psB[:, r % 2, :].rearrange("p (k e) -> p k e", e=P)).then_inc(s_hsTc, 1)
            evac(1, table(1), 4)
            act.wait_ge(s_evac, 8)
            act.dma_start(by_tile(q_ho), T[:, 1, :, :]).then_inc(s_tab[1], 16)

            def exps(g):
                act.wait_ge(s_ed, g + 1)
                nc.scalar.activation(ex[:, :], ed[:, :], ACT.Exp).then_inc(s_ex, 1)

            def table_dyn(i):
                return lambda b: T[:, bass.ds(i, 1), b // 2, b % 2 * HALF:(b % 2 + 1) * HALF]

            exps(0)
            act.wait_ge(s_tab[0], 16)
            act.wait_ge(s_tab[1], 16)
            evac(4, table(0), 4)
            with act.Fori(1, PAIRS - 1) as i:
                exps(2 * i - 1)
                exps(2 * i)
                act.wait_ge(s_wfree, WSLOTS * (i + 5))
                for b in range(4):
                    nc.scalar.copy(T[:, bass.ds(i, 1), b // 2, b % 2 * HALF:(b % 2 + 1) * HALF].rearrange("p a d -> p (a d)"),
                                   psG[:, b, :]).then_inc(s_evac, 1)
            act.dma_start(by_tile(p_oo), T[:, 0, :, :]).then_inc(s_tab[2], 16)
            act.wait_ge(s_boo, NT)
            act.dma_start(by_tile(q_oo), T[:, 1, :, :]).then_inc(s_tab[3], 16)
            exps(2 * PAIRS - 3)
            exps(2 * PAIRS - 2)
            act.wait_ge(s_h, NT)
            evac(9, lambda b: h[:, b // 2, b % 2 * HALF:(b % 2 + 1) * HALF], 4)
            exps(2 * PAIRS - 1)
            exps(2 * PAIRS)
            for j in range(NT):
                act.wait_ge(s_AT, j + 1)
                nc.scalar.copy(AT[:, j, :], psB[:, j, 0:N]).then_inc(s_ATc, 1)
            act.wait_ge(s_ohu, GT * (2 * PAIRS + 1))
            nc.scalar.copy(Wd[:, :, :], psW[:, :, :]).then_inc(s_Wd, 1)
            for t in range(NT):
                act.wait_ge(s_st2, t + 1)
                nc.scalar.activation(sd[:, t:t + 1], mv[:, t, 1:2], ACT.Sqrt, bias=epst[:, 0:1]).then_inc(s_sd2, 1)
                act.wait_ge(s_nb2, t + 1)
                nc.scalar.activation(h2[:, t, :], xs[:, t, 0:N], ACT.Relu, bias=nb[:, t:t + 1],
                                     scale=rs[:, t:t + 1]).then_inc(s_h2, 1)
            for t in range(NT):
                act.wait_ge(s_h2T, t + 1)
                nc.scalar.copy(h2T[:, :, t * P:(t + 1) * P], psB[:, t, 0:N].rearrange("p (j n) -> p j n", n=P)
                               ).then_inc(s_h2Tc, 1)

        @block.vector
        def _(dve):
            steps = [0]

            def chain(ins):
                steps[0] += 1
                ins.then_inc(s_v, 1)
                dve.wait_ge(s_v, steps[0])

            def norm(t, var_sem, sd_sem, nb_sem, count):
                for b in range(2):
                    chain(nc.vector.bn_stats(st[:, t, b, :], xs[:, t, b * HALF:(b + 1) * HALF]))
                nc.vector.bn_aggr(mv[:, t, :], st[:, t, :, :].rearrange("p b s -> p (b s)")).then_inc(var_sem, 1)

            for t in range(NT):
                dve.wait_ge(s_x, 16 * NT)
                norm(t, s_var, None, None, 0)
            dve.wait_ge(s_sd, 1)
            chain(nc.vector.reciprocal(rs[:, :], sd[:, :]))
            nc.vector.scalar_tensor_tensor(out=nb[:, :], in0=mv[:, :, 0], scalar=-1.0, in1=rs[:, :],
                                           op0=ALU.mult, op1=ALU.mult).then_inc(s_nb, 1)
            for b in range(2, 4):
                dve.wait_ge(s_hT, b + 1)
                nc.vector.tensor_copy(hT[:, 2 * b:2 * b + 2, :], psG[:, b, :].rearrange("p (k n) -> p k n", n=N)
                                      ).then_inc(s_hTd, 1)
            dve.wait_ge(s_ewh, 1)
            chain(nc.vector.tensor_tensor(ewl[:, :], ew[:, :], ewh[:, :].bitcast(f32), ALU.subtract))
            dve.wait_ge(s_wa, 16)
            dve.wait_ge(s_small, 64)
            dve.wait_ge(s_const, 1)
            dve.wait_ge(s_pool, 3)
            dve.wait_ge(s_dstb, E // CAST * 16)

            CH = 13

            def rows(g, par, k0, k1, hh=False):
                for k in range(k0, k1):
                    slot = k
                    dve.wait_ge(s_gq[slot], 16 * (g + 1))
                    nc.vector.scalar_tensor_tensor(out=G[:, slot, :], in0=G[:, slot, :], scalar=0.0, in1=wa[:, :],
                                                   op0=ALU.max, op1=ALU.mult, accum_out=lg[:, par, k:k + 1]
                                                   ).then_inc(s_used, 1)

            def logits(g, par, n_used):
                dve.wait_ge(s_used, n_used)
                nc.vector.tensor_scalar(lg[:, par, :], lg[:, par, :], bar[:, 0:1], None, ALU.add).then_inc(s_lg, 1)

            def post1(g, par, base, tile0):
                for c in range(NT):
                    dve_in = dstb[:, bass.ds(tile0 * P, GT * P)]
                    nc.vector.tensor_scalar(eqT[:, par, c, :], dve_in, pid[:, c:c + 1], None, ALU.is_equal
                                            ).then_inc(s_ind, 1)
                    nc.vector.tensor_scalar(negm[:, c, :], dve_in, pid[:, c:c + 1], NEG, ALU.not_equal, ALU.mult
                                            ).then_inc(s_v, 1)
                dve.wait_ge(s_v, base + 2)
                dve.wait_ge(s_bc, g + 1)
                dve.sem_inc(s_rowsok, 1)
                for c in range(NT):
                    nc.vector.tensor_tensor_reduce(
                        out=masked[:, c, :].rearrange("p (a e) -> p a e", a=2), in0=rowsB,
                        in1=negm[:, c, :].rearrange("p (a e) -> p a e", a=2), scale=1.0,
                        scalar=mx[:, 1 - par, c:c + 1], op0=ALU.add, op1=ALU.max,
                        accum_out=mx[:, par, c:c + 1]).then_inc(s_v, 1)
                dve.wait_ge(s_v, base + 4)
                nc.vector.tensor_tensor(ed[:, GT:GT + NT], mx[:, 1 - par, :], mx[:, par, :], ALU.subtract
                                        ).then_inc(s_v, 1)
                nc.vector.tensor_copy(msp[:, :, 0], mx[:, par, :]).then_inc(s_v, 1)
                dve.wait_ge(s_v, base + 6)
                nc.vector.tensor_tensor(mres[:, 0, :], mx[:, par, :], msp[:, :, 0], ALU.subtract).then_inc(s_v, 1)
                dve.wait_ge(s_v, base + 7)
                nc.vector.tensor_copy(msp[:, :, 1], mres[:, 0, :]).then_inc(s_v, 1)
                dve.wait_ge(s_v, base + 8)
                nc.vector.tensor_tensor(mres[:, 1, :], mres[:, 0, :], msp[:, :, 1], ALU.subtract).then_inc(s_v, 1)
                dve.wait_ge(s_v, base + 9)
                nc.vector.tensor_copy(msp[:, :, 2], mres[:, 1, :]).then_inc(s_m, 1)

            def post2(g, par, base):
                dve.wait_ge(s_mg, g + 1)
                nc.vector.tensor_reduce(mg[:, :], psM.rearrange("p (t s) -> p t s", s=3), AX.X, ALU.add
                                        ).then_inc(s_v, 1)
                dve.wait_ge(s_v, base + 10)
                nc.vector.tensor_tensor(ed[:, 0:GT], lg[:, par, :], mg[:, :], ALU.subtract).then_inc(s_ed, 1)
                dve.wait_ge(s_ex, g + 1)
                nc.vector.tensor_copy(exh[:, :], ex[:, 0:GT]).then_inc(s_v, 1)
                dve.wait_ge(s_v, base + 11)
                nc.vector.tensor_tensor(exl[:, :], ex[:, 0:GT], exh[:, :].bitcast(f32), ALU.subtract
                                        ).then_inc(s_v, 1)
                dve.wait_ge(s_v, base + 12)

            def post3(g, tile0, first):
                for k in range(GT):
                    r = k % RING
                    if not (first and k < RING):
                        dve.wait_ge(s_ohu, g * GT + k + 1 - RING)
                    col = bass.ds(tile0 + k, 1)
                    srcs = idf[:, col, 0]
                    nc.vector.tensor_scalar(ohd[:, r, :], iota[:, :], idf[:, col, 1], None, ALU.is_equal)
                    for q, val in enumerate((exh[:, k:k + 1], exl[:, k:k + 1], ewh[:, col], ewl[:, col])):
                        last = nc.vector.tensor_scalar(R[:, r, q, :], iota[:, :], srcs, val.bitcast(f32),
                                                       ALU.is_equal, ALU.mult)
                    last.then_inc(s_oh, 1)

            def post4(g, base):
                dve.wait_ge(s_ohu, GT * (g + 1))
                for c in range(NT):
                    last = nc.vector.scalar_tensor_tensor(out=A[:, c, :], in0=A[:, c, :],
                                                          scalar=ex[:, GT + c:GT + c + 1], in1=psA[:, c, :],
                                                          op0=ALU.mult, op1=ALU.add)
                last.then_inc(s_acc, 1)

            base0 = steps[0]

            def vbase(g):
                return base0 + g * (CH - 1)

            def group(g, par, post):
                tile0 = HO0 + (g - 1) * GT
                rows(g, par, 0, 2)
                if post:
                    if post == "next":
                        dve.wait_ge(s_acc, g - 1)
                    post1(g - 1, 1 - par, vbase(g - 1), tile0)
                rows(g, par, 2, 4)
                if post:
                    post2(g - 1, 1 - par, vbase(g - 1))
                rows(g, par, 4, 5)
                if post:
                    post3(g - 1, tile0, post == "first")
                rows(g, par, 5, 6)
                logits(g, par, (g + 1) * GT)
                if post:
                    post4(g - 1, 0)

            group(0, 0, None)
            dve.wait_ge(s_wfree, WSLOTS * 4)
            nc.vector.scalar_tensor_tensor(out=psG[:, 0:2, :].rearrange("p b d -> p (b d)"),
                                           in0=psG[:, 0:2, :].rearrange("p b d -> p (b d)"), scalar=0.0,
                                           in1=wa[:, :], op0=ALU.max, op1=ALU.mult,
                                           accum_out=lg0[:, 0:1]).then_inc(s_hh, 1)
            group(1, 1, "first")
            with dve.Fori(1, PAIRS - 1) as i:
                group(2 * i, 0, "next")
                group(2 * i + 1, 1, "next")
            dve.wait_ge(s_evac, 8 + 4 * 2)
            for t in range(NT):
                nc.vector.tensor_tensor(T[:, 1, t, :], T[:, 1, t, :], boo[:, :], ALU.add).then_inc(s_boo, 1)
            group(2 * PAIRS - 2, 0, "next")
            group(2 * PAIRS - 1, 1, "next")
            g = 2 * PAIRS
            dve.wait_ge(s_acc, g - 1)
            post1(g - 1, 1, vbase(g - 1), HO0 + (g - 1) * GT)
            dve.wait_ge(s_hh, 1)
            nc.vector.tensor_copy(lg[:, 0, 0:1], lg0[:, :]).then_inc(s_used, 1)
            post2(g - 1, 1, vbase(g - 1))
            post3(g - 1, HO0 + (g - 1) * GT, False)
            for j in range(OO_TILES):
                dve.wait_ge(s_gq[j], 16 * (g + 1))
                nc.vector.scalar_tensor_tensor(out=G[:, j, :], in0=G[:, j, :], scalar=0.0, in1=wa[:, :],
                                               op0=ALU.max, op1=ALU.mult, accum_out=lg[:, 0, j + 1:j + 2]
                                               ).then_inc(s_used, 1)
            logits(g, 0, HO_TILES + GT)
            post4(g - 1, 0)
            dve.wait_ge(s_acc, g)
            post1(g, 0, vbase(g), 0)
            post2(g, 0, vbase(g))
            post3(g, 0, False)
            post4(g, 0)
            steps[0] = vbase(g + 1)
            dve.wait_ge(s_acc, g + 1)
            chain(nc.vector.tensor_reduce(den[:, :], A[:, :, :], AX.X, ALU.add))
            chain(nc.vector.tensor_scalar(den[:, :], den[:, :], 0.5, None, ALU.max))
            chain(nc.vector.reciprocal(den[:, :], den[:, :]))
            dve.wait_ge(s_up, 1)
            dve.wait_ge(s_evac, 8 + 4 * 5)
            for t in range(NT):
                prod = psG[:, 2 * t:2 * t + 2, :].rearrange("p b d -> p (b d)")
                chain(nc.vector.scalar_tensor_tensor(out=G[:, t, :], in0=prod, scalar=den[:, t:t + 1],
                                                     in1=h[:, t, :], op0=ALU.mult, op1=ALU.add))
                chain(nc.vector.scalar_tensor_tensor(out=xs[:, t, :], in0=G[:, t, :], scalar=0.0, in1=xs[:, t, :],
                                                     op0=ALU.max, op1=ALU.add))
                norm(t, s_st2, None, None, 0)
            for t in range(NT):
                dve.wait_ge(s_sd2, t + 1)
                chain(nc.vector.reciprocal(rs[:, t:t + 1], sd[:, t:t + 1]))
                nc.vector.scalar_tensor_tensor(out=nb[:, t:t + 1], in0=mv[:, t, 0:1], scalar=-1.0,
                                               in1=rs[:, t:t + 1], op0=ALU.mult, op1=ALU.mult).then_inc(s_nb2, 1)
            for t in range(NT):
                dve.wait_ge(s_h2, t + 1)
                chain(nc.vector.tensor_tensor(xs[:, t, :], xs[:, t, :], lb[:, :], ALU.add))
            for t in range(NT):
                dve.wait_ge(s_y, t + 1)
                nc.vector.tensor_tensor(xs[:, t, 0:N], xs[:, t, 0:N], (psA, psW)[t][:, 0, :], ALU.add).then_inc(s_o, 1)

        @block.tensor
        def _(pe):
            pe.wait_ge(s_const, 1)
            pe.wait_ge(s_h, NT)
            for b in range(4):
                for q in range(4):
                    k, t = 2 * b + q // 2, q % 2
                    last = nc.tensor.transpose(psG[:, b, q * P:(q + 1) * P], h[:, t, k * P:(k + 1) * P], ident[:, :])
                last.then_inc(s_hT, 1)
            nc.tensor.matmul(psW[:, :, :].rearrange("p c n -> p (c n)"), zero[:, 0:P], zero[:, :],
                             start=True, stop=False, skip_group_check=True)
            pe.wait_ge(s_hTc, 2)
            pe.wait_ge(s_hTd, 2)

            def chunk(lap, k, tiles, first, last):
                if k % 2 == 0:
                    pe.wait_ge(s_w[k // 2], 16 * (lap + 1))
                for lhs, rows, bank in tiles:
                    for half in range(2):
                        ins = nc.tensor.matmul(psG[rows, bank + half, :], lhs(k),
                                               W[:, k // 2, k % 2, half * HALF:(half + 1) * HALF],
                                               start=first and k == 0, stop=last and k == KC - 1)
                if k % 2 == 1:
                    ins.then_inc(s_wfree, 1)

            def bias(row, tiles):
                for _, rows, bank in tiles:
                    m = rows.stop - rows.start
                    for half in range(2):
                        nc.tensor.matmul(psG[rows, bank + half, :], sel[:, row, 0:m],
                                         brow[:, half * HALF:(half + 1) * HALF], start=True, stop=False)

            every = slice(0, P)
            nodes = [(lambda k, t=t: hT[:, k, t * P:(t + 1) * P], every, 2 * t) for t in range(NT)]

            for k in range(KC):
                chunk(0, k, nodes, True, True)
            for r in range(4):
                if r % 2 == 0:
                    pe.wait_ge(s_hg[r // 2], 16)
                if r >= 2:
                    pe.wait_ge(s_hsTc, r - 1)
                for q in range(4):
                    k = 4 * (r % 2) + q
                    last = nc.tensor.transpose(psB[:, r % 2, q * P:(q + 1) * P], G[:, r // 2, k * P:(k + 1) * P],
                                               ident[:, :])
                last.then_inc(s_hsT, 1)
            pe.wait_ge(s_small, 64)
            pe.wait_ge(s_evac, 4)
            bias(0, nodes)
            for k in range(KC):
                chunk(1, k, nodes, False, True)
            pe.wait_ge(s_hsTc, 4)
            pe.wait_ge(s_evac, 8)
            for c in range(2):
                ends = [(lambda k, c=c: hsT[:, c, k, :], every, 0)]
                if c == 0:
                    bias(1, ends)
                for k in range(KC):
                    chunk(2 + c, k, ends, False, c == 1)

            def spread(g, par):
                pe.wait_ge(s_lg, g + 1)
                for k in range(GT):
                    a, q = divmod(k, GT // 2)
                    last = nc.tensor.matmul(psB[:, a, q * P:(q + 1) * P],
                                            lg[:, par, k:k + 1].broadcast_to((P, P)), ident[:, :],
                                            start=True, stop=True)
                last.then_inc(s_bc, 1)

            def edge_max(g, par):
                pe.wait_ge(s_ind, (g + 1) * 2)
                pe.wait_ge(s_m, g + 1)
                for k in range(GT):
                    for c in range(NT):
                        last = nc.tensor.matmul(psM[:, 3 * k:3 * k + 3], eqT[:, par, c, k * P:(k + 1) * P],
                                                msp[:, c, :], start=c == 0, stop=c == NT - 1)
                last.then_inc(s_mg, 1)

            def sums(g, first):
                if not first:
                    pe.wait_ge(s_acc, g)
                nc.tensor.matmul(psA[:, :, :].rearrange("p c n -> p (c n)"), zero[:, 0:P], zero[:, :],
                                 start=True, stop=False, skip_group_check=True)
                for k in range(GT):
                    pe.wait_ge(s_oh, g * GT + k + 1)
                    for c in range(NT):
                        for q in range(4):
                            ins = nc.tensor.matmul((psA if q < 2 else psW)[:, c, :],
                                                   ohd[:, k % RING, c * P:(c + 1) * P], R[:, k % RING, q, :],
                                                   start=False, stop=False, skip_group_check=True)
                    ins.then_inc(s_ohu, 1)

            def pair(i, first):
                lap = i + 4
                pe.wait_ge(s_evac, 8 + 4 * i) if not first else pe.wait_ge(s_hh, 1)
                if not first:
                    spread(2 * i - 1, 1)
                chunk(lap, 0, nodes, True, True)
                chunk(lap, 1, nodes, True, True)
                if not first:
                    edge_max(2 * i - 1, 1)
                chunk(lap, 2, nodes, True, True)
                if not first:
                    sums(2 * i - 1, False)
                chunk(lap, 3, nodes, True, True)
                spread(2 * i, 0)
                chunk(lap, 4, nodes, True, True)
                chunk(lap, 5, nodes, True, True)
                edge_max(2 * i, 0)
                chunk(lap, 6, nodes, True, True)
                sums(2 * i, first)
                chunk(lap, 7, nodes, True, True)

            pair(0, True)
            with pe.Fori(1, PAIRS - 1) as i:
                pair(i, False)
            i = PAIRS - 1
            low, high = slice(0, NH), slice(NH, P)
            hn = [(lambda k: hT[:, k, 0:NH], low, 0)]
            on = [(lambda k: hT[:, k, NH:P], high, 0), (lambda k: hT[:, k, P:N], every, 2)]
            pe.wait_ge(s_evac, 8 + 4 * i)
            bias(2, hn)
            bias(3, on)
            spread(2 * i - 1, 1)
            for k in range(4):
                chunk(8, k, hn, False, True)
            edge_max(2 * i - 1, 1)
            for k in range(4, 8):
                chunk(8, k, hn, False, True)
            sums(2 * i - 1, False)
            spread(2 * i, 0)
            for k in range(3):
                chunk(9, k, on, False, True)
            edge_max(2 * i, 0)
            for k in range(3, 6):
                chunk(9, k, on, False, True)
            sums(2 * i, False)
            for k in range(6, 8):
                chunk(9, k, on, False, True)
            for g in (2 * PAIRS - 1, 2 * PAIRS):
                spread(g, g % 2)
                edge_max(g, g % 2)
                sums(g, False)
            pe.wait_ge(s_acc, 2 * PAIRS + 1)
            for j in range(NT):
                for c in range(NT):
                    last = nc.tensor.transpose(psB[:, j, c * P:(c + 1) * P], A[:, c, j * P:(j + 1) * P], ident[:, :])
                last.then_inc(s_AT, 1)
            pe.wait_ge(s_ATc, NT)
            pe.wait_ge(s_evac, 8 + 4 * 5)
            for rows, bank, v, cols in ((low, 0, 2, slice(0, NH)), (high, 0, 3, slice(NH, P)), (every, 2, 3, slice(P, N))):
                for half in range(2):
                    for j in range(NT):
                        last = nc.tensor.matmul(psG[rows, bank + half, :], AT[:, j, cols],
                                                T[:, v, j, half * HALF:(half + 1) * HALF],
                                                start=j == 0, stop=j == NT - 1)
            last.then_inc(s_up, 1)
            for t in range(NT):
                pe.wait_ge(s_h2, t + 1)
                for j in range(NT):
                    last = nc.tensor.transpose(psB[:, t, j * P:(j + 1) * P], h2[:, t, j * P:(j + 1) * P], ident[:, :])
                last.then_inc(s_h2T, 1)
            pe.wait_ge(s_Wd, 1)
            for t in range(NT):
                pe.wait_ge(s_h2Tc, t + 1)
                for j in range(NT):
                    last = nc.tensor.matmul((psA, psW)[t][:, 0, :], h2T[:, j, t * P:(t + 1) * P], Wd[:, j, :],
                                            start=j == 0, stop=j == NT - 1)
                last.then_inc(s_y, 1)


def kernel(**inputs):
    import numpy as np
    import concourse.bacc as bacc
    from concourse.bass_utils import run_bass_kernel_spmd

    a = {k: np.asarray(v) for k, v in inputs.items()}
    D_ = 1024
    top = lambda w: a[f"L0_gnn_W_{w}"][:D_]
    bot = lambda w: a[f"L0_gnn_W_{w}"][D_:]
    cols = lambda v: v.reshape(-1, 128).T
    arrays = {
        "x": a["x"],
        "edge_ids": np.ascontiguousarray(np.stack([cols(a["src"]), cols(a["dst"])], axis=2)),
        "dst_row": np.ascontiguousarray(a["dst"].reshape(1, -1)),
        "edge_w": np.ascontiguousarray(cols(a["edge_weight"])),
        "weights": np.ascontiguousarray(np.concatenate(
            [top("ho"), bot("ho"), top("hh"), bot("hh"), top("oo"), bot("oo"), bot("hn"), bot("on"),
             top("hn"), top("on")])),
        "bias_rows": np.ascontiguousarray(np.stack([a[f"L0_gnn_b_{w}"] for w in ("ho", "hh", "hn", "on")])),
        "b_oo": a["L0_gnn_b_oo"].reshape(1, -1),
        "w_a": np.ascontiguousarray(a["L0_gnn_W_a"].reshape(1, -1)),
        "b_a": a["L0_gnn_b_a"].reshape(1, 1),
        "l1_bias": a["L1_gnn_bias"].reshape(1, -1),
    }
    nc = bacc.Bacc("TRN2", target_bir_lowering=False, num_devices=1)
    aps = [nc.dram_tensor(k, v.shape, mybir.dt.from_np(v.dtype), kind="ExternalInput").ap() for k, v in arrays.items()]
    out = nc.dram_tensor("out", a["x"].shape, mybir.dt.float32, kind="ExternalOutput").ap()
    gnn_block(nc, *aps, out)
    return run_bass_kernel_spmd(nc, [arrays], core_ids=[0]).results[0]["out"]
```

```python
import concourse.bass as bass
from concourse import mybir
from contextlib import ExitStack

P = 128
N = 256
NT = N // P
D = 1024
KC = D // P
HALF = 512
E = 8448
ET = E // P
NH = 64
GT = 6
OO_TILES = 5
HO0 = 1 + OO_TILES
HO_TILES = ET - HO0
PAIRS = HO_TILES // (2 * GT)
VT = 2
UNITS = 10
WSLOTS = 4
STEP = WSLOTS
STEP0 = UNITS * KC - 2 * PAIRS * STEP
LAG = 3
RING = 3
SLOTS = 2 * GT
BIASES = 5
LOW0 = 32
NEG = -3.0e38
EPS = 1e-5
TAIL = (1, 0)
HH_AFTER = (4, 5, 6, 7)
CAST = 1056


def gnn_block(nc, x, edge_ids, dst_row, edge_w, weights, bias_rows, w_a, b_a, l1_bias, out):
    f32, f32r, bf16, i32 = mybir.dt.float32, mybir.dt.float32r, mybir.dt.bfloat16, mybir.dt.int32
    ALU = mybir.AluOpType
    ACT = mybir.ActivationFunctionType
    AX = mybir.AxisListType

    h_rows = nc.dram_tensor("h_rows", (N, D), f32, kind="Internal").ap()
    p_ho = nc.dram_tensor("p_ho", (N, D), f32, kind="Internal").ap()
    q_ho = nc.dram_tensor("q_ho", (N, D), f32, kind="Internal").ap()
    p_oo = nc.dram_tensor("p_oo", (N, D), f32, kind="Internal").ap()
    q_oo = nc.dram_tensor("q_oo", (N, D), f32, kind="Internal").ap()
    by_tile = lambda t: t.rearrange("(a p) d -> p a d", p=P)

    ctx = ExitStack()
    with ctx:
        sb = lambda name, shape, dt: ctx.enter_context(nc.sbuf_tensor(name, shape, dt))
        pb = lambda name, shape, dt: ctx.enter_context(nc.psum_tensor(name, shape, dt))
        sem = lambda name: ctx.enter_context(nc.semaphore(name))

        def shared(*makes):
            with ExitStack() as part:
                return [part.enter_context(nc.sbuf_tensor(*m)) for m in makes]

        _, hsh, hsl = shared(("t_low", [P, 2, NT, D], f32), ("hsh", [P, 2, KC, P], f32r),
                             ("hsl", [P, 2, KC, P], f32r))
        x1, AT, Wd, h2, h2T = shared(("x1", [P, NT, D], f32), ("AT", [P, NT, N], f32), ("Wd", [P, NT, N], f32),
                                     ("h2", [P, NT, N], f32), ("h2T", [P, NT, N], f32))
        T = sb("T", [P, 4, NT, D], f32)
        W = sb("W", [P, WSLOTS, D], f32)
        Wh = sb("Wh", [P, WSLOTS, D], f32r)
        Wl = sb("Wl", [P, WSLOTS, D], f32r)
        hTh = sb("hTh", [P, KC, N], f32r)
        hTl = sb("hTl", [P, KC, N], f32r)
        xs, h = shared(("xs", [P, NT, D], f32), ("h", [P, NT, D], f32))
        G = sb("G", [P, SLOTS, D], f32)
        wa = sb("wa", [P, D], f32)
        brep = sb("brep", [P, D], f32)
        biases = sb("biases", [LOW0 + 32, D], f32r)
        selr = sb("selr", [LOW0 + 32, BIASES, P], f32r)
        ids = sb("ids", [P, ET, 2], i32)
        idf = sb("idf", [P, ET, 2], f32)
        ewh = sb("ewh", [P, ET], f32r)
        ewl = sb("ewl", [P, ET], f32r)
        stage_p = sb("stage_p", [P, 2 * GT], i32)
        stage_q = sb("stage_q", [P, 2 * GT], i32)
        stage_h = sb("stage_h", [P, 2], i32)
        dstb = sb("dstb", [P, E], bf16)
        brow, sel, ew = shared(("brow", [LOW0 + 32, D], f32), ("sel", [LOW0 + 32, BIASES, P], f32),
                               ("ew", [P, ET], f32))
        eqT = sb("eqT", [P, 2, NT, GT * P], bf16)
        negm = sb("negm", [P, NT, GT * P], bf16)
        ident = sb("ident", [P, P], f32)
        iota = sb("iota", [P, N], f32)
        pid = sb("pid", [P, NT], f32)
        zero = sb("zero", [P, HALF], bf16)
        bar = sb("bar", [P, 1], f32)
        st = sb("st", [P, NT, 2, 6], f32)
        mv = sb("mv", [P, NT, 2], f32)
        sd = sb("sd", [P, NT], f32)
        rs = sb("rs", [P, NT], f32)
        nb = sb("nb", [P, NT], f32)
        epst = sb("epst", [P, 1], f32)
        warm = sb("warm", [P, 1], f32)
        lg = sb("lg", [P, 2, GT], f32)
        lg0 = sb("lg0", [P, 1], f32)
        mx = sb("mx", [P, 2, NT], f32)
        mres = sb("mres", [P, 2, NT], f32)
        msp = sb("msp", [P, NT, 3], bf16)
        mg = sb("mg", [P, GT], f32)
        ed = sb("ed", [P, 2, GT + NT], f32)
        ex = sb("ex", [P, 2, GT + NT], f32)
        exh = sb("exh", [P, 2, GT], f32r)
        exl = sb("exl", [P, 2, GT], f32r)
        ohd = sb("ohd", [P, RING, N], f32r)
        ohs = sb("ohs", [P, RING, N], bf16)
        R = sb("R", [P, RING, 4, N], f32r)
        A = sb("A", [P, NT, N], f32)
        den = sb("den", [P, NT], f32)

        psG = pb("psG", [P, 4, HALF], f32)
        psB = pb("psB", [P, 2, HALF], f32)
        psA = pb("psA", [P, NT, N], f32)
        psW = pb("psW", [P, NT, N], f32)
        psM = psB[:, 0, GT // 2 * P:GT // 2 * P + 3 * GT]
        rowsB = psB[:, :, 0:GT // 2 * P]
        hT_banks = [psB[:, 0, :], psB[:, 1, :], psA[:, :, :].rearrange("p c n -> p (c n)"),
                    psW[:, :, :].rearrange("p c n -> p (c n)")]

        s_x, s_ids, s_ew, s_wa, s_small, s_dstb = map(sem, ("x_in", "ids_in", "ew_in", "wa_in", "small_in", "dstb_in"))
        s_w = [sem(f"w_in{i}") for i in range(WSLOTS)]
        s_hi, s_lo, s_wused = sem("w_high_made"), sem("w_low_made"), sem("w_used")
        s_hTl, s_hsTl = sem("hT_low"), sem("hsT_low")
        s_ohs, s_prod = sem("src_onehot"), sem("src_products")
        s_lb = sem("l1_bias_in")
        s_const, s_pool = sem("const_made"), sem("pool_step")
        s_hst, s_hg = sem("h_stored"), [sem("hsrc_in"), sem("hdst_in")]
        s_tab = [sem("p_ho_stored"), sem("q_ho_stored"), sem("p_oo_stored"), sem("q_oo_stored")]
        s_gp = [sem(f"p_rows{i}") for i in range(SLOTS)]
        s_gq = [sem(f"q_rows{i}") for i in range(SLOTS)]
        s_claim = sem("slot_claimed")
        s_used = sem("rows_used")
        s_v = sem("vector_step")
        s_h, s_hT, s_hTc = sem("h_made"), sem("hT_made"), sem("hT_copied")
        s_hsT, s_hsTc = sem("hsT_made"), sem("hsT_copied")
        s_evac = sem("unit_copied")
        s_ewh, s_bh, s_bl = sem("weights_high"), sem("biases_high"), sem("biases_low")
        s_hh = sem("hh_logit")
        s_lg, s_bc, s_m, s_mg = sem("logits_ready"), sem("logit_rows"), sem("max_ready"), sem("edge_max")
        s_ed, s_ex = sem("exp_in"), sem("exp_out")
        s_oh, s_ohu = sem("onehot_ready"), sem("onehot_used")
        s_acc = sem("group_added")
        s_alpha = sem("A_over_den")
        s_xlo, s_ylo = sem("x_again"), sem("tail_columns_ready")
        s_AT, s_ATc, s_up = sem("AT_made"), sem("AT_copied"), sem("update_made")
        s_Wd, s_st2, s_sd2, s_nb2, s_h2 = sem("Wd_copied"), sem("var2"), sem("std2"), sem("norm2"), sem("h2_made")
        s_h2T, s_h2Tc, s_y, s_o, s_out = sem("h2T_made"), sem("h2T_copied"), sem("y_made"), sem("out_ready"), sem("out_stored")
        s_var, s_sd, s_nb = sem("var1"), sem("std1"), sem("norm1")
        s_ind = sem("onehotT_ready")
        s_rowsok = sem("rows_claimed")

        block = ctx.enter_context(nc.Block())

        @block.sync
        def _(sp):
            for t in range(NT):
                sp.dma_start(xs[:, t, :], by_tile(x)[:, t, :]).then_inc(s_x, 16)
            sp.dma_start(ids[:, :, :], edge_ids).then_inc(s_ids, 16)

            def load(v, s):
                row = (v * WSLOTS + s) * P
                sp.dma_start(W[:, s, :], weights[bass.ds(row, P), :]).then_inc(s_w[s], 16)

            for s in range(WSLOTS):
                load(0, s)
            sp.dma_start(ew[:, :], edge_w).then_inc(s_ew, 16)
            sp.wait_ge(s_const, 1)
            for p0 in (0, LOW0):
                sp.dma_start(brow[p0:p0 + BIASES, :], bias_rows).then_inc(s_small, 16)
            sp.dma_start(bar[:, :], b_a.broadcast_to((P, 1))).then_inc(s_small, 16)
            for s in range(WSLOTS):
                sp.wait_ge(s_lo, s + 1)
                load(1, s)
            sp.dma_start(wa[:, :], w_a.broadcast_to((P, D))).then_inc(s_wa, 16)
            with sp.Fori(2, UNITS * KC // WSLOTS) as v:
                for s in range(WSLOTS):
                    sp.wait_ge(s_lo, v * WSLOTS + s + 1 - WSLOTS)
                    load(v, s)
            sp.dma_start(brep[:, :], l1_bias.broadcast_to((P, D))).then_inc(s_lb, 16)
            sp.wait_ge(s_tab[2], 16)
            sp.dma_start(x1[:, :, :], by_tile(x)).then_inc(s_xlo, 16)
            for n, t in enumerate(TAIL):
                sp.wait_ge(s_ylo, n + 1)
                sp.dma_start(by_tile(out)[:, t, N:D], x1[:, t, N:D]).then_inc(s_out, 16)
            for n, t in enumerate(TAIL):
                sp.wait_ge(s_o, n + 1)
                sp.dma_start(by_tile(out)[:, t, 0:N], x1[:, t, 0:N]).then_inc(s_out, 16)
            sp.wait_ge(s_out, 16 * 2 * NT)

        @block.gpsimd
        def _(pool):
            nc.gpsimd.memset(ident[:, :], 0.0).then_inc(s_pool, 1)
            nc.gpsimd.memset(sel[:, :, :], 0.0).then_inc(s_pool, 1)
            nc.gpsimd.memset(brow[:, :], 0.0).then_inc(s_pool, 1)
            nc.gpsimd.memset(zero[:, :], 0.0)
            nc.gpsimd.memset(epst[:, :], EPS)
            nc.gpsimd.memset(A[:, :, :], 0.0)
            nc.gpsimd.memset(mx[:, 1, :], NEG)
            nc.gpsimd.iota(iota[:, :], pattern=[[1, N]], base=0, channel_multiplier=0,
                           allow_small_or_imprecise_dtypes=True)
            nc.gpsimd.iota(pid[:, :], pattern=[[P, NT]], base=0, channel_multiplier=1,
                           allow_small_or_imprecise_dtypes=True)
            pool.wait_ge(s_pool, 3)
            nc.gpsimd.affine_select(out=ident[:, :], in_=ident[:, :], compare_op=ALU.not_equal, fill=1.0, base=0,
                                    pattern=[[-1, P]], channel_multiplier=1)
            nc.gpsimd.affine_select(out=sel[:, :, :], in_=sel[:, :, :], compare_op=ALU.not_equal, fill=1.0, base=0,
                                    pattern=[[-1, BIASES], [0, P]], channel_multiplier=1).then_inc(s_pool, 1)
            pool.wait_ge(s_pool, 4)
            nc.gpsimd.affine_select(out=sel[:, :, :], in_=sel[:, :, :], compare_op=ALU.not_equal, fill=1.0, base=-LOW0,
                                    pattern=[[-1, BIASES], [0, P]], channel_multiplier=1).then_inc(s_const, 1)
            pool.wait_ge(s_ids, 16)
            nc.gpsimd.tensor_copy(stage_h[:, :], ids[:, 0, :])
            nc.gpsimd.tensor_copy(stage_p[:, :], ids[:, HO0:HO0 + 2 * GT, 0])
            nc.gpsimd.tensor_copy(stage_q[:, :], ids[:, HO0:HO0 + 2 * GT, 1])
            nc.gpsimd.tensor_copy(idf[:, :, :], ids[:, :, :]).then_inc(s_pool, 1)
            pool.wait_ge(s_pool, 5)
            pool.wait_ge(s_hst, 16)
            for c in range(2):
                nc.gpsimd.indirect_dma_start(out=G[:, SLOTS - 2 + c, :], out_offset=None, in_=h_rows,
                                             in_offset=bass.IndirectOffsetOnAxis(ap=stage_h[:, c:c + 1], axis=0)
                                             ).then_inc(s_hg[c], 16)
            for c in range(E // CAST):
                pool.dma_start(dstb[:, c * CAST:(c + 1) * CAST],
                               dst_row[:, c * CAST:(c + 1) * CAST].broadcast_to((P, CAST))).then_inc(s_dstb, 16)

            def p_rows(slot, table):
                nc.gpsimd.indirect_dma_start(out=G[:, slot, :], out_offset=None, in_=table,
                                             in_offset=bass.IndirectOffsetOnAxis(ap=stage_p[:, slot:slot + 1], axis=0)
                                             ).then_inc(s_gp[slot], 16)

            def q_rows(lap, slot, table):
                pool.wait_ge(s_gp[slot], 16 * (lap + 1))
                pool.sem_inc(s_claim, 1)
                nc.gpsimd.indirect_dma_start(out=G[:, slot, :], out_offset=None, in_=table,
                                             in_offset=bass.IndirectOffsetOnAxis(ap=stage_q[:, slot:slot + 1], axis=0),
                                             compute_op=ALU.add).then_inc(s_gq[slot], 16)

            def pair(i, first, last):
                n0 = SLOTS * i
                lag = SLOTS if first else LAG
                for j in range(SLOTS):
                    if not first:
                        pool.wait_ge(s_used, n0 + j + 1 - SLOTS)
                        pool.sem_inc(s_claim, 1)
                    elif j == 0:
                        pool.wait_ge(s_tab[0], 16)
                        pool.wait_ge(s_hT, 4)
                    elif j == SLOTS - 2:
                        pool.wait_ge(s_hsT, 4)
                    p_rows(j, p_ho)
                    if j == LAG - 1 and not first:
                        for k in range(SLOTS):
                            pool.wait_ge(s_gq[k], 16 * i)
                        pool.sem_inc(s_claim, 1)
                        nc.gpsimd.tensor_copy(stage_q[:, :], ids[:, bass.ds(HO0 + n0, SLOTS), 1]
                                              ).then_inc(s_pool, 1)
                        pool.wait_ge(s_pool, 5 + 2 * i)
                        pool.sem_inc(s_claim, 1)
                    if j >= lag:
                        q_rows(i, j - lag, q_ho)
                if first:
                    pool.wait_ge(s_tab[1], 16)
                for k in range(SLOTS - lag, SLOTS):
                    q_rows(i, k, q_ho)
                if not last:
                    nc.gpsimd.tensor_copy(stage_p[:, :], ids[:, bass.ds(HO0 + n0 + SLOTS, SLOTS), 0]
                                          ).then_inc(s_pool, 1)
                    pool.wait_ge(s_pool, 6 + 2 * i)
                    pool.sem_inc(s_claim, 1)

            pair(0, True, False)
            with pool.Fori(1, PAIRS - 1) as i:
                pair(i, False, False)
            pair(PAIRS - 1, False, True)
            nc.gpsimd.tensor_copy(stage_p[:, 0:OO_TILES], ids[:, 1:HO0, 0]).then_inc(s_pool, 1)
            for k in range(SLOTS):
                pool.wait_ge(s_gq[k], 16 * PAIRS)
            nc.gpsimd.tensor_copy(stage_q[:, 0:OO_TILES], ids[:, 1:HO0, 1]).then_inc(s_pool, 1)
            pool.wait_ge(s_pool, 5 + 2 * (PAIRS - 1) + 2)
            pool.wait_ge(s_tab[2], 16)
            pool.wait_ge(s_tab[3], 16)
            for j in range(OO_TILES):
                pool.wait_ge(s_used, HO_TILES + j + 1 - SLOTS)
                p_rows(j, p_oo)
            for j in range(OO_TILES):
                q_rows(PAIRS, j, q_oo)

        @block.scalar
        def _(act):
            act.wait_ge(s_var, NT)
            act.wait_ge(s_const, 1)
            nc.scalar.activation(sd[:, :], mv[:, :, 1], ACT.Sqrt, bias=epst[:, 0:1]).then_inc(s_sd, 1)
            for t in range(NT):
                act.wait_ge(s_nb, 1)
                nc.scalar.activation(h[:, t, :], xs[:, t, :], ACT.Relu, bias=nb[:, t:t + 1],
                                     scale=rs[:, t:t + 1]).then_inc(s_h, 1)
            act.wait_ge(s_h, NT)
            act.dma_start(by_tile(h_rows), h[:, :, :]).then_inc(s_hst, 16)
            def high(q, slot, lap, first=False):
                act.wait_ge(s_w[slot], 16 * (lap + 1))
                if not first:
                    act.wait_ge(s_wused, q - WSLOTS + 1)
                nc.scalar.copy(Wh[:, slot, :], W[:, slot, :]).then_inc(s_hi, 1)

            def highs(q0, q1):
                for q in range(q0, q1):
                    high(q, q % WSLOTS, q // WSLOTS, first=q < WSLOTS)

            def evac(u, banks):
                act.wait_ge(s_wused, KC * (u + 1))
                for dst, src in banks:
                    nc.scalar.copy(dst, src).then_inc(s_evac, 1)

            def banks_to(tile):
                return [(tile[:, b // 2, b % 2 * HALF:(b % 2 + 1) * HALF], psG[:, b, :]) for b in range(4)]

            def hs_high(r):
                act.wait_ge(s_hsT, r + 1)
                nc.scalar.copy(hsh[:, r // 2, 4 * (r % 2):4 * (r % 2) + 4, :],
                               psB[:, r % 2, :].rearrange("p (k e) -> p k e", e=P)).then_inc(s_hsTc, 1)

            for b in range(4):
                highs(b, b + 1)
                act.wait_ge(s_hT, b + 1)
                nc.scalar.copy(hTh[:, 2 * b:2 * b + 2, :], hT_banks[b].rearrange("p (k n) -> p k n", n=N)
                               ).then_inc(s_hTc, 1)
            act.wait_ge(s_ew, 16)
            nc.scalar.copy(ewh[:, :], ew[:, :]).then_inc(s_ewh, 1)
            act.wait_ge(s_small, 48)
            nc.scalar.copy(biases[:, :], brow[:, :]).then_inc(s_bh, 1)
            act.wait_ge(s_const, 1)
            nc.scalar.copy(selr[:, :, :], sel[:, :, :]).then_inc(s_bh, 1)
            for r in range(4):
                highs(4 + 2 * r, 6 + 2 * r)
                hs_high(r)
            evac(0, banks_to(T[:, 0, :, :]))
            act.wait_ge(s_evac, 4)
            act.dma_start(by_tile(p_ho), T[:, 0, :, :]).then_inc(s_tab[0], 16)
            highs(KC + 4, 2 * KC + 3)
            evac(1, banks_to(T[:, 1, :, :]))
            act.wait_ge(s_evac, 8)
            act.dma_start(by_tile(q_ho), T[:, 1, :, :]).then_inc(s_tab[1], 16)
            highs(2 * KC + 3, 4 * KC + 4)

            def exps(g, par):
                act.wait_ge(s_ed, g + 1)
                nc.scalar.activation(ex[:, par, :], ed[:, par, :], ACT.Exp).then_inc(s_ex, 1)

            def products(g, par, tile0, k0, k1, parts=(0, 1, 2, 3)):
                for k in range(k0, k1):
                    act.wait_ge(s_ohs, g * GT + k + 1)
                    col = bass.ds(tile0 + k, 1)
                    for q in parts:
                        val = (exh[:, par, k:k + 1], exl[:, par, k:k + 1], ewh[:, col], ewl[:, col])[q]
                        last = nc.scalar.activation(R[:, k % RING, q, :], ohs[:, k % RING, :], ACT.Copy,
                                                    scale=val.bitcast(f32))
                    last.then_inc(s_prod, 1)

            def step(g, par, tile0, last=False):
                q0, lap = STEP0 + g * STEP, g + STEP0 // STEP
                products(g, par, tile0, 0, 3)
                high(q0 + 2, 2, lap)
                products(g, par, tile0, 3, 4)
                high(q0 + 3, 3, lap)
                products(g, par, tile0, 4, 5)
                exps(g + 1, 1 - par)
                if not last:
                    high(q0 + STEP, 0, lap + 1)
                products(g, par, tile0, 5, GT)
                if not last:
                    high(q0 + STEP + 1, 1, lap + 1)

            exps(0, 0)
            highs(4 * KC + 4, STEP0 + 2)
            act.wait_ge(s_tab[0], 16)
            evac(4, banks_to(T[:, 0, :, :]))
            act.wait_ge(s_evac, 12)
            act.dma_start(by_tile(p_oo), T[:, 0, :, :]).then_inc(s_tab[2], 16)
            step(0, 0, HO0)
            step(1, 1, HO0 + GT)
            act.wait_ge(s_tab[1], 16)
            evac(5, banks_to(T[:, 1, :, :]))
            act.wait_ge(s_evac, 16)
            act.dma_start(by_tile(q_oo), T[:, 1, :, :]).then_inc(s_tab[3], 16)
            with act.Fori(1, 1 + VT) as j:
                for r in range(2):
                    step(2 * j + r, r, HO0 + (2 * j + r) * GT)
                act.wait_ge(s_wused, KC * (j + 6))
                for b in range(4):
                    nc.scalar.copy(T[:, bass.ds(j + 1, 1), b // 2, b % 2 * HALF:(b % 2 + 1) * HALF].rearrange("p a d -> p (a d)"),
                                   psG[:, b, :]).then_inc(s_evac, 1)
            for g in range(2 + 2 * VT, 2 * PAIRS):
                step(g, g % 2, HO0 + g * GT, last=g == 2 * PAIRS - 1)
            nc.scalar.activation(warm[:, :], epst[:, :], ACT.Sqrt)
            products(g + 1, 0, 0, 0, GT, parts=(2, 3))
            act.wait_ge(s_tab[3], 16)
            act.wait_ge(s_ohu, GT * (2 * PAIRS + 1))
            nc.scalar.copy(Wd[:, :, :], psW[:, :, :]).then_inc(s_Wd, 1)
            for j in range(NT):
                act.wait_ge(s_AT, j + 1)
                nc.scalar.copy(AT[:, j, :], psB[:, j, 0:N]).then_inc(s_ATc, 1)
            for n, t in enumerate(TAIL):
                act.wait_ge(s_st2, n + 1)
                nc.scalar.activation(sd[:, t:t + 1], mv[:, t, 1:2], ACT.Sqrt, bias=epst[:, 0:1]).then_inc(s_sd2, 1)
                act.wait_ge(s_nb2, n + 1)
                nc.scalar.activation(h2[:, t, :], x1[:, t, 0:N], ACT.Relu, bias=nb[:, t:t + 1],
                                     scale=rs[:, t:t + 1]).then_inc(s_h2, 1)
                act.wait_ge(s_h2T, n + 1)
                nc.scalar.copy(h2T[:, :, t * P:(t + 1) * P], psB[:, t, 0:N].rearrange("p (j n) -> p j n", n=P)
                               ).then_inc(s_h2Tc, 1)

        @block.vector
        def _(dve):
            steps = [0]

            def chain(ins):
                steps[0] += 1
                ins.then_inc(s_v, 1)
                dve.wait_ge(s_v, steps[0])

            def norm(rows, t, var_sem):
                for b in range(2):
                    chain(nc.vector.bn_stats(st[:, t, b, :], rows[:, t, b * HALF:(b + 1) * HALF]))
                nc.vector.bn_aggr(mv[:, t, :], st[:, t, :, :].rearrange("p b s -> p (b s)")).then_inc(var_sem, 1)

            for t in range(NT):
                dve.wait_ge(s_x, 16 * NT)
                norm(xs, t, s_var)
            dve.wait_ge(s_sd, 1)
            chain(nc.vector.reciprocal(rs[:, :], sd[:, :]))
            nc.vector.scalar_tensor_tensor(out=nb[:, :], in0=mv[:, :, 0], scalar=-1.0, in1=rs[:, :],
                                           op0=ALU.mult, op1=ALU.mult).then_inc(s_nb, 1)
            def low(q, slot):
                dve.wait_ge(s_hi, q + 1)
                nc.vector.tensor_tensor(Wl[:, slot, :], W[:, slot, :], Wh[:, slot, :].bitcast(f32), ALU.subtract
                                        ).then_inc(s_lo, 1)

            def lows(q0, q1):
                for q in range(q0, q1):
                    low(q, q % WSLOTS)

            for b in range(4):
                lows(b, b + 1)
                dve.wait_ge(s_hTc, b + 1)
                nc.vector.tensor_tensor(hTl[:, 2 * b:2 * b + 2, :], hT_banks[b].rearrange("p (k n) -> p k n", n=N),
                                        hTh[:, 2 * b:2 * b + 2, :].bitcast(f32), ALU.subtract).then_inc(s_hTl, 1)
            dve.wait_ge(s_bh, 2)
            low_rows = slice(LOW0, LOW0 + 32)
            nc.vector.tensor_tensor(biases[low_rows, :], brow[low_rows, :], biases[low_rows, :].bitcast(f32),
                                    ALU.subtract).then_inc(s_bl, 1)
            for r in range(4):
                lows(4 + 2 * r, 6 + 2 * r)
                dve.wait_ge(s_hsTc, r + 1)
                nc.vector.tensor_tensor(hsl[:, r // 2, 4 * (r % 2):4 * (r % 2) + 4, :],
                                        psB[:, r % 2, :].rearrange("p (k e) -> p k e", e=P),
                                        hsh[:, r // 2, 4 * (r % 2):4 * (r % 2) + 4, :].bitcast(f32), ALU.subtract
                                        ).then_inc(s_hsTl, 1)
            dve.wait_ge(s_ewh, 1)
            chain(nc.vector.tensor_tensor(ewl[:, :], ew[:, :], ewh[:, :].bitcast(f32), ALU.subtract))
            lows(KC + 4, 2 * KC)
            dve.wait_ge(s_wa, 16)
            dve.wait_ge(s_small, 48)
            dve.wait_ge(s_const, 1)
            dve.wait_ge(s_pool, 5)
            dve.wait_ge(s_dstb, E // CAST * 16)

            CH = 13

            def rows(lap, par, k0, k1):
                for k in range(k0, k1):
                    slot = par * GT + k
                    dve.wait_ge(s_gq[slot], 16 * (lap + 1))
                    nc.vector.scalar_tensor_tensor(out=G[:, slot, :], in0=G[:, slot, :], scalar=0.0, in1=wa[:, :],
                                                   op0=ALU.max, op1=ALU.mult, accum_out=lg[:, par, k:k + 1]
                                                   ).then_inc(s_used, 1)

            def logits(g, par, n_used):
                dve.wait_ge(s_used, n_used)
                nc.vector.tensor_scalar(lg[:, par, :], lg[:, par, :], bar[:, 0:1], None, ALU.add).then_inc(s_lg, 1)

            def post1(g, par, base, tile0):
                for c in range(NT):
                    dve_in = dstb[:, bass.ds(tile0 * P, GT * P)]
                    nc.vector.tensor_scalar(eqT[:, par, c, :], dve_in, pid[:, c:c + 1], None, ALU.is_equal
                                            ).then_inc(s_ind, 1)
                    nc.vector.tensor_scalar(negm[:, c, :], dve_in, pid[:, c:c + 1], NEG, ALU.not_equal, ALU.mult
                                            ).then_inc(s_v, 1)
                dve.wait_ge(s_v, base + 2)
                dve.wait_ge(s_bc, g + 1)
                dve.sem_inc(s_rowsok, 1)
                for c in range(NT):
                    nc.vector.tensor_tensor_reduce(
                        out=negm[:, c, :].rearrange("p (a e) -> p a e", a=2), in0=rowsB,
                        in1=negm[:, c, :].rearrange("p (a e) -> p a e", a=2), scale=1.0,
                        scalar=mx[:, 1 - par, c:c + 1], op0=ALU.add, op1=ALU.max,
                        accum_out=mx[:, par, c:c + 1]).then_inc(s_v, 1)
                dve.wait_ge(s_v, base + 4)
                nc.vector.tensor_tensor(ed[:, par, GT:GT + NT], mx[:, 1 - par, :], mx[:, par, :], ALU.subtract
                                        ).then_inc(s_v, 1)
                nc.vector.tensor_copy(msp[:, :, 0], mx[:, par, :]).then_inc(s_v, 1)
                dve.wait_ge(s_v, base + 6)
                nc.vector.tensor_tensor(mres[:, 0, :], mx[:, par, :], msp[:, :, 0], ALU.subtract).then_inc(s_v, 1)
                dve.wait_ge(s_v, base + 7)
                nc.vector.tensor_copy(msp[:, :, 1], mres[:, 0, :]).then_inc(s_v, 1)
                dve.wait_ge(s_v, base + 8)
                nc.vector.tensor_tensor(mres[:, 1, :], mres[:, 0, :], msp[:, :, 1], ALU.subtract).then_inc(s_v, 1)
                dve.wait_ge(s_v, base + 9)
                nc.vector.tensor_copy(msp[:, :, 2], mres[:, 1, :]).then_inc(s_m, 1)

            def post2(g, par, base):
                dve.wait_ge(s_mg, g + 1)
                nc.vector.tensor_reduce(mg[:, :], psM.rearrange("p (t s) -> p t s", s=3), AX.X, ALU.add
                                        ).then_inc(s_v, 1)
                dve.wait_ge(s_v, base + 10)
                nc.vector.tensor_tensor(ed[:, par, 0:GT], lg[:, par, :], mg[:, :], ALU.subtract).then_inc(s_ed, 1)

            def post3(g, par, base):
                dve.wait_ge(s_ex, g + 1)
                nc.vector.tensor_copy(exh[:, par, :], ex[:, par, 0:GT]).then_inc(s_v, 1)
                dve.wait_ge(s_v, base + 11)
                nc.vector.tensor_tensor(exl[:, par, :], ex[:, par, 0:GT], exh[:, par, :].bitcast(f32), ALU.subtract
                                        ).then_inc(s_v, 1)
                dve.wait_ge(s_v, base + 12)

            def onehot(g, tile0, k, par=0, first=False, parts=()):
                r = k % RING
                if not (first and k < RING):
                    dve.wait_ge(s_ohu, g * GT + k + 1 - RING)
                col = bass.ds(tile0 + k, 1)
                nc.vector.tensor_scalar(ohs[:, r, :], iota[:, :], idf[:, col, 0], None, ALU.is_equal
                                        ).then_inc(s_ohs, 1)
                for q in parts:
                    val = (exh[:, par, k:k + 1], exl[:, par, k:k + 1])[q]
                    nc.vector.tensor_scalar(R[:, r, q, :], iota[:, :], idf[:, col, 0], val.bitcast(f32),
                                            ALU.is_equal, ALU.mult)
                nc.vector.tensor_scalar(ohd[:, r, :], iota[:, :], idf[:, col, 1], None, ALU.is_equal
                                        ).then_inc(s_oh, 1)

            def add(g, par, first=False, sums=False):
                dve.wait_ge(s_ohu, GT * (g + 1))
                if not first:
                    dve.wait_ge(s_acc, g)
                for c in range(NT):
                    last = nc.vector.scalar_tensor_tensor(out=A[:, c, :], in0=A[:, c, :],
                                                          scalar=ex[:, par, GT + c:GT + c + 1], in1=psA[:, c, :],
                                                          op0=ALU.mult, op1=ALU.add,
                                                          **({"accum_out": den[:, c:c + 1]} if sums else {}))
                last.then_inc(s_acc, 1)

            base0 = steps[0]

            def vbase(g):
                return base0 + g * (CH - 1)

            def step(g, par, row, chunks, tile0_next=None, first=False, second=False):
                tile0 = HO0 + g * GT
                nxt, at = 1 - par, vbase(g + 1)

                def lowered(n):
                    for q, slot in chunks[n]:
                        low(q, slot)

                lowered(0)
                row(0)
                if not first:
                    add(g - 1, nxt, second)
                onehot(g, tile0, 0, first=first)
                post1(g + 1, nxt, at, tile0 + GT if tile0_next is None else tile0_next)
                onehot(g, tile0, 1, first=first)
                onehot(g, tile0, 2, first=first)
                lowered(1)
                row(1)
                onehot(g, tile0, 3)
                row(2)
                post2(g + 1, nxt, at)
                onehot(g, tile0, 4)
                row(3)
                onehot(g, tile0, 5)
                lowered(2)
                row(4)
                post3(g + 1, nxt, at)
                lowered(3)
                row(5)

            pieces = lambda g: [[(STEP0 + g * STEP + s, s)] for s in range(STEP)]

            def loop_step(g, j, par, **more):
                step(g, par, lambda k: rows(j + 1, par, k, k + 1),
                     pieces(g), **more)
                logits(g + 2, par, (g + 3) * GT)

            lows(2 * KC, 3 * KC)
            for k in range(GT):
                rows(0, 0, k, k + 1)
                lows(3 * KC + 2 * k, min(3 * KC + 2 * k + 2, 4 * KC))
            logits(0, 0, GT)
            dve.wait_ge(s_wused, KC * 4)
            nc.vector.scalar_tensor_tensor(out=psG[:, 0:2, :].rearrange("p b d -> p (b d)"),
                                           in0=psG[:, 0:2, :].rearrange("p b d -> p (b d)"), scalar=0.0,
                                           in1=wa[:, :], op0=ALU.max, op1=ALU.mult,
                                           accum_out=lg0[:, 0:1]).then_inc(s_hh, 1)
            p_low = lambda k: low(4 * KC + k, k % WSLOTS)
            p_low(0)
            post1(0, 0, vbase(0), HO0)
            for k in range(3):
                p_low(1 + k)
                rows(0, 1, k, k + 1)
            post2(0, 0, vbase(0))
            for k in range(3):
                p_low(4 + k)
                rows(0, 1, 3 + k, 4 + k)
            post3(0, 0, vbase(0))
            p_low(7)
            logits(1, 1, 2 * GT)
            loop_step(0, 0, 0, first=True)
            loop_step(1, 0, 1, second=True)
            with dve.Fori(1, 1 + VT) as j:
                loop_step(2 * j, j, 0)
                loop_step(2 * j + 1, j, 1)
            j = 1 + VT
            loop_step(2 * j, j, 0)
            loop_step(2 * j + 1, j, 1)
            g = 2 * PAIRS - 2

            def last_rows(k):
                if k == 0:
                    nc.vector.tensor_copy(lg[:, 0, 0:1], lg0[:, :]).then_inc(s_used, 1)
                    return
                dve.wait_ge(s_gq[k - 1], 16 * (PAIRS + 1))
                nc.vector.scalar_tensor_tensor(out=G[:, k - 1, :], in0=G[:, k - 1, :], scalar=0.0, in1=wa[:, :],
                                               op0=ALU.max, op1=ALU.mult, accum_out=lg[:, 0, k:k + 1]
                                               ).then_inc(s_used, 1)

            step(g, 0, last_rows, pieces(g))
            logits(g + 2, 0, HO_TILES + GT)
            step(g + 1, 1, lambda k: None, pieces(g + 1), tile0_next=0)
            g = 2 * PAIRS
            onehot(g, 0, 0, parts=(0, 1))
            add(g - 1, 1)
            for k in range(1, GT):
                onehot(g, 0, k, parts=(0, 1))
            add(g, 0, sums=True)
            steps[0] = vbase(g + 1)
            dve.wait_ge(s_acc, g + 1)
            chain(nc.vector.tensor_scalar(den[:, :], den[:, :], 0.5, None, ALU.max))
            chain(nc.vector.reciprocal(den[:, :], den[:, :]))
            for c in range(NT):
                nc.vector.tensor_scalar(A[:, c, :], A[:, c, :], den[:, c:c + 1], None, ALU.mult).then_inc(s_alpha, 1)
            dve.wait_ge(s_lb, 16)
            dve.wait_ge(s_xlo, 16)
            for n, t in enumerate(TAIL):
                for half in range(2):
                    cols = slice(half * HALF, (half + 1) * HALF)
                    dve.wait_ge(s_up, 2 * n + half + 1)
                    chain(nc.vector.scalar_tensor_tensor(out=x1[:, t, cols], in0=psG[:, 2 * t + half, :], scalar=0.0,
                                                         in1=x1[:, t, cols], op0=ALU.max, op1=ALU.add))
                    chain(nc.vector.bn_stats(st[:, t, half, :], x1[:, t, cols]))
                nc.vector.bn_aggr(mv[:, t, :], st[:, t, :, :].rearrange("p b s -> p (b s)")).then_inc(s_st2, 1)
                dve.wait_ge(s_sd2, n + 1)
                chain(nc.vector.reciprocal(rs[:, t:t + 1], sd[:, t:t + 1]))
                nc.vector.scalar_tensor_tensor(out=nb[:, t:t + 1], in0=mv[:, t, 0:1], scalar=-1.0,
                                               in1=rs[:, t:t + 1], op0=ALU.mult, op1=ALU.mult).then_inc(s_nb2, 1)
            for n, t in enumerate(TAIL):
                nc.vector.tensor_tensor(x1[:, t, N:D], x1[:, t, N:D], brep[:, N:D], ALU.add).then_inc(s_ylo, 1)
                dve.wait_ge(s_h2, n + 1)
                chain(nc.vector.tensor_tensor(x1[:, t, 0:N], x1[:, t, 0:N], brep[:, 0:N], ALU.add))
            for n, t in enumerate(TAIL):
                dve.wait_ge(s_y, n + 1)
                nc.vector.tensor_tensor(x1[:, t, 0:N], x1[:, t, 0:N], (psW, psA)[t][:, 0, :], ALU.add).then_inc(s_o, 1)

        @block.tensor
        def _(pe):
            pe.wait_ge(s_const, 1)
            pe.wait_ge(s_h, NT)
            for b in range(4):
                for q in range(4):
                    k, t = 2 * b + q // 2, q % 2
                    last = nc.tensor.transpose(hT_banks[b][:, q * P:(q + 1) * P], h[:, t, k * P:(k + 1) * P], ident[:, :])
                last.then_inc(s_hT, 1)

            def free(bank, copied):
                if copied is not None:
                    pe.wait_ge(s_evac, copied + bank + 1)

            def chunk(q, k, tiles, opened=False, last=True, copied=None):
                pe.wait_ge(s_lo, q + 1)
                s = k % WSLOTS
                for high, low, rows, bank in tiles:
                    passes = ((high, Wh), (high, Wl), (low, Wh))
                    for n, (lhs, rhs) in enumerate(passes):
                        for half in range(2):
                            if k == 0 and n == 0:
                                free(bank + half, copied)
                            ins = nc.tensor.matmul(psG[rows, bank + half, :], lhs(k),
                                                   rhs[:, s, half * HALF:(half + 1) * HALF],
                                                   start=not opened and k == 0 and n == 0,
                                                   stop=last and k == KC - 1 and n == 2)
                ins.then_inc(s_wused, 1)

            def bias(row, tiles, copied=None):
                for _, _, rows, bank in tiles:
                    for half in range(2):
                        free(bank + half, copied)
                        nc.tensor.matmul(psG[rows, bank + half, :], selr[:, row, rows],
                                         biases[:, half * HALF:(half + 1) * HALF], start=True, stop=False)

            def node_tile(rows, t):
                cols = slice(t * P + rows.start, t * P + rows.stop)
                return (lambda k: hTh[:, k, cols], lambda k: hTl[:, k, cols], rows, 2 * t)

            nodes = [node_tile(slice(0, P), t) for t in range(NT)]

            for k in range(KC):
                if k % 2 == 0:
                    pe.wait_ge(s_hTl, k // 2 + 1)
                chunk(k, k, nodes)
                if k == 3:
                    pe.wait_ge(s_hTl, 4)
                    nc.tensor.matmul(psW[:, :, :].rearrange("p c n -> p (c n)"), zero[:, 0:P], zero[:, :],
                                     start=True, stop=False, skip_group_check=True)
                if k in HH_AFTER:
                    r = HH_AFTER.index(k)
                    if r % 2 == 0:
                        pe.wait_ge(s_hg[r // 2], 16)
                    if r >= 2:
                        pe.wait_ge(s_hsTl, r - 1)
                    for q in range(4):
                        kk = 4 * (r % 2) + q
                        last = nc.tensor.transpose(psB[:, r % 2, q * P:(q + 1) * P],
                                                   G[:, SLOTS - 2 + r // 2, kk * P:(kk + 1) * P], ident[:, :])
                    last.then_inc(s_hsT, 1)
            pe.wait_ge(s_bl, 1)
            pe.wait_ge(s_bh, 2)
            bias(0, nodes, copied=0)
            for k in range(KC):
                chunk(KC + k, k, nodes, opened=True)
            pe.wait_ge(s_hsTl, 4)
            for c in range(2):
                ends = [(lambda k, c=c: hsh[:, c, k, :], lambda k, c=c: hsl[:, c, k, :], slice(0, P), 0)]
                if c == 0:
                    bias(1, ends, copied=4)
                for k in range(KC):
                    chunk((2 + c) * KC + k, k, ends, opened=True, last=c == 1)

            def spread(g, par):
                pe.wait_ge(s_lg, g + 1)
                for k in range(GT):
                    a, q = divmod(k, GT // 2)
                    last = nc.tensor.matmul(psB[:, a, q * P:(q + 1) * P],
                                            lg[:, par, k:k + 1].broadcast_to((P, P)), ident[:, :],
                                            start=True, stop=True)
                last.then_inc(s_bc, 1)

            def edge_max(g, par):
                pe.wait_ge(s_ind, (g + 1) * 2)
                pe.wait_ge(s_m, g + 1)
                for k in range(GT):
                    for c in range(NT):
                        last = nc.tensor.matmul(psM[:, 3 * k:3 * k + 3], eqT[:, par, c, k * P:(k + 1) * P],
                                                msp[:, c, :], start=c == 0, stop=c == NT - 1)
                last.then_inc(s_mg, 1)

            def sums(g, k0, k1, first=False):
                if k0 == 0:
                    if not first:
                        pe.wait_ge(s_acc, g)
                    nc.tensor.matmul(psA[:, :, :].rearrange("p c n -> p (c n)"), zero[:, 0:P], zero[:, :],
                                     start=True, stop=False, skip_group_check=True)
                for k in range(k0, k1):
                    pe.wait_ge(s_oh, g * GT + k + 1)
                    pe.wait_ge(s_prod, g * GT + k + 1)
                    for c in range(NT):
                        for q in range(4):
                            ins = nc.tensor.matmul((psA if q < 2 else psW)[:, c, :],
                                                   ohd[:, k % RING, c * P:(c + 1) * P], R[:, k % RING, q, :],
                                                   start=False, stop=False, skip_group_check=True)
                    ins.then_inc(s_ohu, 1)

            def step(g, par, q, k0, tiles=nodes, row=None, copied=None, first=False):
                def chunks(n):
                    chunk(q + n, k0 + n, tiles, opened=row is not None, copied=copied if row is None else None)

                spread(g + 1, 1 - par)
                if row is not None and k0 == 0:
                    bias(row, tiles, copied)
                chunks(0)
                sums(g, 0, 3, first)
                edge_max(g + 1, 1 - par)
                chunks(1)
                sums(g, 3, GT)
                chunks(2)
                chunks(3)

            spread(0, 0)
            pe.wait_ge(s_hh, 1)
            for k in range(KC):
                chunk(4 * KC + k, k, nodes, copied=4)
                if k == 3:
                    edge_max(0, 0)
            copied = lambda j: 8 + 4 * j
            q = lambda g: STEP0 + g * STEP
            step(0, 0, q(0), 0, row=4, copied=copied(0), first=True)
            step(1, 1, q(1), STEP, row=4)
            with pe.Fori(1, 1 + VT) as j:
                step(2 * j, 0, q(2 * j), 0, copied=copied(j))
                step(2 * j + 1, 1, q(2 * j + 1), STEP)
            g = 2 + 2 * VT
            step(g, 0, q(g), 0, row=3, copied=copied(1 + VT))
            step(g + 1, 1, q(g + 1), STEP, row=3)
            heads = [node_tile(slice(0, NH), 0)]
            step(g + 2, 0, q(g + 2), 0, tiles=heads, row=2)
            step(g + 3, 1, q(g + 3), STEP, tiles=heads, row=2)
            g += 2
            sums(g + 2, 0, GT)
            for j in range(NT):
                for c in range(NT):
                    pe.wait_ge(s_alpha, c + 1)
                    last = nc.tensor.transpose(psB[:, j, c * P:(c + 1) * P], A[:, c, j * P:(j + 1) * P], ident[:, :])
                last.then_inc(s_AT, 1)
            pe.wait_ge(s_ATc, NT)
            pe.wait_ge(s_evac, 8 + 4 * 4)
            for t, parts in ((1, ((slice(0, P), 3),)), (0, ((slice(0, NH), 2), (slice(NH, P), 3)))):
                for half in range(2):
                    for rows, v in parts:
                        for j in range(NT):
                            last = nc.tensor.matmul(psG[rows, 2 * t + half, :],
                                                    AT[:, j, t * P + rows.start:t * P + rows.stop],
                                                    T[:, v, j, half * HALF:(half + 1) * HALF],
                                                    start=False, stop=j == NT - 1,
                                                    skip_group_check=True)
                    last.then_inc(s_up, 1)
            pe.wait_ge(s_Wd, 1)
            for n, t in enumerate(TAIL):
                pe.wait_ge(s_h2, n + 1)
                for j in range(NT):
                    last = nc.tensor.transpose(psB[:, t, j * P:(j + 1) * P], h2[:, t, j * P:(j + 1) * P], ident[:, :])
                last.then_inc(s_h2T, 1)
                pe.wait_ge(s_h2Tc, n + 1)
                for j in range(NT):
                    last = nc.tensor.matmul((psW, psA)[t][:, 0, :], h2T[:, j, t * P:(t + 1) * P], Wd[:, j, :],
                                            start=j == 0, stop=j == NT - 1)
                last.then_inc(s_y, 1)


def kernel(**inputs):
    import numpy as np
    import concourse.bacc as bacc
    from concourse.bass_utils import run_bass_kernel_spmd

    a = {k: np.asarray(v) for k, v in inputs.items()}
    D_ = 1024
    top = lambda w: a[f"L0_gnn_W_{w}"][:D_]
    bot = lambda w: a[f"L0_gnn_W_{w}"][D_:]
    cols = lambda v: v.reshape(-1, 128).T
    arrays = {
        "x": a["x"],
        "edge_ids": np.ascontiguousarray(np.stack([cols(a["src"]), cols(a["dst"])], axis=2)),
        "dst_row": np.ascontiguousarray(a["dst"].reshape(1, -1)),
        "edge_w": np.ascontiguousarray(cols(a["edge_weight"])),
        "weights": np.ascontiguousarray(np.concatenate(
            [top("ho"), bot("ho"), top("hh"), bot("hh"), top("oo"), bot("oo"), bot("hn"), bot("on"),
             top("on"), top("hn")])),
        "bias_rows": np.ascontiguousarray(np.stack([a[f"L0_gnn_b_{w}"] for w in ("ho", "hh", "hn", "on", "oo")])),
        "w_a": np.ascontiguousarray(a["L0_gnn_W_a"].reshape(1, -1)),
        "b_a": a["L0_gnn_b_a"].reshape(1, 1),
        "l1_bias": a["L1_gnn_bias"].reshape(1, -1),
    }
    nc = bacc.Bacc("TRN2", target_bir_lowering=False, num_devices=1)
    aps = [nc.dram_tensor(k, v.shape, mybir.dt.from_np(v.dtype), kind="ExternalInput").ap() for k, v in arrays.items()]
    out = nc.dram_tensor("out", a["x"].shape, mybir.dt.float32, kind="ExternalOutput").ap()
    gnn_block(nc, *aps, out)
    return run_bass_kernel_spmd(nc, [arrays], core_ids=[0]).results[0]["out"]
```

```python
import concourse.bass as bass
from concourse import mybir
from contextlib import ExitStack

P = 128
N = 256
NT = N // P
D = 1024
KC = D // P
HALF = 512
E = 8448
ET = E // P
NH = 64
GT = 6
OO_TILES = 5
HO0 = 1 + OO_TILES
HO_TILES = ET - HO0
PAIRS = HO_TILES // (2 * GT)
VT = 2
UNITS = 10
WSLOTS = 4
FAN_FIRST = 4
STEP = WSLOTS
STEP0 = UNITS * KC - 2 * PAIRS * STEP
LAG = 3
RING = 3
EARLY = 2 * GT
SLOTS = 2 * GT
BIASES = 5
LOW0 = 32
END = EARLY + (2 * PAIRS - 1) * GT
EARLY_TILES = list(range(ET - GT, ET)) + list(range(GT))
NEG = -3.0e38
EPS = 1e-5
TAIL = (1, 0)
HH_AFTER = KC
WARM = 10


def gnn_block(nc, x, edge_ids, dst_row, edge_w, weights, bias_rows, w_a, b_a, l1_bias, out):
    f32, f32r, bf16, i32 = mybir.dt.float32, mybir.dt.float32r, mybir.dt.bfloat16, mybir.dt.int32
    ALU = mybir.AluOpType
    ACT = mybir.ActivationFunctionType
    AX = mybir.AxisListType

    h_rows = nc.dram_tensor("h_rows", (N, D), f32, kind="Internal").ap()
    p_ho = nc.dram_tensor("p_ho", (N, D), f32, kind="Internal").ap()
    q_ho = nc.dram_tensor("q_ho", (N, D), f32, kind="Internal").ap()
    p_oo = nc.dram_tensor("p_oo", (N, D), f32, kind="Internal").ap()
    q_oo = nc.dram_tensor("q_oo", (N, D), f32, kind="Internal").ap()
    by_tile = lambda t: t.rearrange("(a p) d -> p a d", p=P)

    ctx = ExitStack()
    with ctx:
        sb = lambda name, shape, dt: ctx.enter_context(nc.sbuf_tensor(name, shape, dt))
        pb = lambda name, shape, dt: ctx.enter_context(nc.psum_tensor(name, shape, dt))
        sem = lambda name: ctx.enter_context(nc.semaphore(name))

        def shared(*makes):
            with ExitStack() as part:
                return [part.enter_context(nc.sbuf_tensor(*m)) for m in makes]

        _, hsh, hsl = shared(("t_low", [P, 2, NT, D], f32), ("hsh", [P, 2, KC, P], f32r),
                             ("hsl", [P, 2, KC, P], f32r))
        x1, AT, Wd, h2, h2T = shared(("x1", [P, NT, D], f32), ("AT", [P, NT, N], f32), ("Wd", [P, NT, N], f32),
                                     ("h2", [P, NT, N], f32), ("h2T", [P, NT, N], f32))
        T = sb("T", [P, 4, NT, D], f32)
        W = sb("W", [P, WSLOTS, D], f32)
        Wh = sb("Wh", [P, WSLOTS, D], f32r)
        Wl = sb("Wl", [P, WSLOTS, D], f32r)
        hTh = sb("hTh", [P, KC, N], f32r)
        hTl = sb("hTl", [P, KC, N], f32r)
        xs, h = shared(("xs", [P, NT, D], f32), ("h", [P, NT, D], f32))
        _, ohs_end, ohd_end = shared(("g_low", [P, GT, D], f32), ("ohs_end", [P, EARLY, N], bf16),
                                     ("ohd_end", [P, EARLY, N], f32r))
        G = sb("G", [P, SLOTS, D], f32)
        wa = sb("wa", [P, D], f32)
        brep = sb("brep", [P, D], f32)
        biases = sb("biases", [LOW0 + 32, D], f32r)
        selr = sb("selr", [LOW0 + 32, BIASES, P], f32r)
        ids = sb("ids", [P, ET, 2], i32)
        idf = sb("idf", [P, ET, 2], f32)
        ewh = sb("ewh", [P, ET], f32r)
        ewl = sb("ewl", [P, ET], f32r)
        stage_p = sb("stage_p", [P, 2 * GT], i32)
        stage_q = sb("stage_q", [P, 2 * GT], i32)
        stage_h = sb("stage_h", [P, 2], i32)
        dstb = sb("dstb", [P, E], bf16)
        brow, sel, ew, one = shared(("brow", [LOW0 + 32, D], f32), ("sel", [LOW0 + 32, BIASES, P], f32),
                               ("ew", [P, ET], f32), ("one", [1, P], bf16))
        eqT = sb("eqT", [P, 2, NT, GT * P], bf16)
        negm = sb("negm", [P, NT, GT * P], bf16)
        ident = sb("ident", [P, P], f32)
        iota = sb("iota", [P, N], f32)
        pid = sb("pid", [P, NT], f32)
        zero = sb("zero", [P, HALF], bf16)
        bar = sb("bar", [P, 1], f32)
        st = sb("st", [P, NT, 2, 6], f32)
        mv = sb("mv", [P, NT, 2], f32)
        sd = sb("sd", [P, NT], f32)
        rs = sb("rs", [P, NT], f32)
        nb = sb("nb", [P, NT], f32)
        epst = sb("epst", [P, 1], f32)
        warm = sb("warm", [P, 1], f32)
        lg = sb("lg", [P, 2, GT], f32)
        lg0 = sb("lg0", [P, 1], f32)
        mx = sb("mx", [P, 2, NT], f32)
        mres = sb("mres", [P, 2, NT], f32)
        msp = sb("msp", [P, NT, 3], bf16)
        mg = sb("mg", [P, GT], f32)
        ed = sb("ed", [P, 2, GT + NT], f32)
        ex = sb("ex", [P, 2, GT + NT], f32)
        exh = sb("exh", [P, 2, GT], f32r)
        exl = sb("exl", [P, 2, GT], f32r)
        ohd = sb("ohd", [P, RING, N], f32r)
        ohs = sb("ohs", [P, RING, N], bf16)
        R = sb("R", [P, RING, 4, N], f32r)
        A = sb("A", [P, NT, N], f32)
        den = sb("den", [P, NT], f32)

        psG = pb("psG", [P, 4, HALF], f32)
        psB = pb("psB", [P, 2, HALF], f32)
        psA = pb("psA", [P, NT, N], f32)
        psW = pb("psW", [P, NT, N], f32)
        end_place = lambda i, part: R[:, i % GT // 2, 2 * (i % 2) + part, :]
        psM = psB[:, 0, GT // 2 * P:GT // 2 * P + 3 * GT]
        rowsB = psB[:, :, 0:GT // 2 * P]
        hT_banks = [psB[:, 0, :], psB[:, 1, :], psA[:, :, :].rearrange("p c n -> p (c n)"),
                    psW[:, :, :].rearrange("p c n -> p (c n)")]

        fan = [slice(c, min(c + HALF, E)) for c in range(0, E, HALF)]

        def fan_bank(m):
            bank = psG[:, m, :] if m < FAN_FIRST else psA[:, :, :].rearrange("p c n -> p (c n)")
            return bank[:, 0:fan[m].stop - fan[m].start]

        s_one, s_fan, s_fanc = sem("ones_made"), sem("dst_fanned"), sem("dst_copied")
        s_x = [sem(f"x_in{t}") for t in range(NT)]
        s_ids, s_ew, s_wa, s_small, s_dstb = map(sem, ("ids_in", "ew_in", "wa_in", "small_in", "dstb_in"))
        s_w = [sem(f"w_in{i}") for i in range(WSLOTS)]
        s_hi, s_lo, s_wused = sem("w_high_made"), sem("w_low_made"), sem("w_used")
        s_hTl, s_hsTl = sem("hT_low"), sem("hsT_low")
        s_oh_end, s_exs = sem("end_onehots"), sem("exp_split")
        s_ohs, s_prod = sem("src_onehot"), sem("src_products")
        s_lb = sem("l1_bias_in")
        s_const, s_pool = sem("const_made"), sem("pool_step")
        s_hst, s_hg = sem("h_stored"), [sem("hsrc_in"), sem("hdst_in")]
        s_tab = [sem("p_ho_stored"), sem("q_ho_stored"), sem("p_oo_stored"), sem("q_oo_stored")]
        s_gp = [sem(f"p_rows{i}") for i in range(SLOTS)]
        s_gq = [sem(f"q_rows{i}") for i in range(SLOTS)]
        s_claim = sem("slot_claimed")
        s_used = sem("rows_used")
        s_v = sem("vector_step")
        s_h, s_hT, s_hTc = sem("h_made"), sem("hT_made"), sem("hT_copied")
        s_hsT, s_hsTc = sem("hsT_made"), sem("hsT_copied")
        s_evac = sem("unit_copied")
        s_ewh, s_bh, s_bl = sem("weights_high"), sem("biases_high"), sem("biases_low")
        s_hh = sem("hh_logit")
        s_lg, s_bc, s_m, s_mg = sem("logits_ready"), sem("logit_rows"), sem("max_ready"), sem("edge_max")
        s_ed, s_ex = sem("exp_in"), sem("exp_out")
        s_oh, s_ohu = sem("onehot_ready"), sem("onehot_used")
        s_acc = sem("group_added")
        s_alpha = sem("A_over_den")
        s_xlo, s_ylo = sem("x_again"), sem("tail_columns_ready")
        s_AT, s_ATc, s_up = sem("AT_made"), sem("AT_copied"), sem("update_made")
        s_Wd, s_st2, s_sd2, s_nb2, s_h2 = sem("Wd_copied"), sem("var2"), sem("std2"), sem("norm2"), sem("h2_made")
        s_h2T, s_h2Tc, s_y, s_o, s_out = sem("h2T_made"), sem("h2T_copied"), sem("y_made"), sem("out_ready"), sem("out_stored")
        s_var, s_sd, s_nb = sem("var1"), sem("std1"), sem("norm1")
        s_ind = sem("onehotT_ready")
        s_rowsok = sem("rows_claimed")

        block = ctx.enter_context(nc.Block())

        @block.sync
        def _(sp):
            for t in range(NT):
                sp.dma_start(xs[:, t, :], by_tile(x)[:, t, :]).then_inc(s_x[t], 16)
            sp.dma_start(ids[:, :, :], edge_ids).then_inc(s_ids, 16)

            def load(v, s):
                row = (v * WSLOTS + s) * P
                sp.dma_start(W[:, s, :], weights[bass.ds(row, P), :]).then_inc(s_w[s], 16)

            for s in range(WSLOTS):
                load(0, s)
            sp.dma_start(ew[:, :], edge_w).then_inc(s_ew, 16)
            sp.wait_ge(s_const, 1)
            for p0 in (0, LOW0):
                sp.dma_start(brow[p0:p0 + BIASES, :], bias_rows).then_inc(s_small, 16)
            sp.dma_start(bar[:, :], b_a.broadcast_to((P, 1))).then_inc(s_small, 16)
            for s in range(WSLOTS):
                sp.wait_ge(s_lo, s + 1)
                load(1, s)
            sp.dma_start(wa[:, :], w_a.broadcast_to((P, D))).then_inc(s_wa, 16)
            with sp.Fori(2, UNITS * KC // WSLOTS) as v:
                for s in range(WSLOTS):
                    sp.wait_ge(s_lo, v * WSLOTS + s + 1 - WSLOTS)
                    load(v, s)
            sp.dma_start(brep[:, :], l1_bias.broadcast_to((P, D))).then_inc(s_lb, 16)
            sp.wait_ge(s_tab[2], 16)
            sp.dma_start(x1[:, :, :], by_tile(x)).then_inc(s_xlo, 16)
            for n, t in enumerate(TAIL):
                sp.wait_ge(s_ylo, n + 1)
                sp.dma_start(by_tile(out)[:, t, N:D], x1[:, t, N:D]).then_inc(s_out, 16)
            for n, t in enumerate(TAIL):
                sp.wait_ge(s_o, n + 1)
                sp.dma_start(by_tile(out)[:, t, 0:N], x1[:, t, 0:N]).then_inc(s_out, 16)
            sp.wait_ge(s_out, 16 * 2 * NT)

        @block.gpsimd
        def _(pool):
            pool.dma_start(dstb[0:1, :], dst_row).then_inc(s_dstb, 16)
            nc.gpsimd.memset(one[:, :], 1.0).then_inc(s_one, 1)
            nc.gpsimd.memset(ident[:, :], 0.0).then_inc(s_pool, 1)
            nc.gpsimd.memset(sel[:, :, :], 0.0).then_inc(s_pool, 1)
            nc.gpsimd.memset(brow[:, :], 0.0).then_inc(s_pool, 1)
            nc.gpsimd.memset(zero[:, :], 0.0)
            nc.gpsimd.memset(epst[:, :], EPS)
            nc.gpsimd.memset(A[:, :, :], 0.0)
            nc.gpsimd.memset(mx[:, 1, :], NEG)
            nc.gpsimd.iota(iota[:, :], pattern=[[1, N]], base=0, channel_multiplier=0,
                           allow_small_or_imprecise_dtypes=True)
            nc.gpsimd.iota(pid[:, :], pattern=[[P, NT]], base=0, channel_multiplier=1,
                           allow_small_or_imprecise_dtypes=True)
            pool.wait_ge(s_pool, 3)
            nc.gpsimd.affine_select(out=ident[:, :], in_=ident[:, :], compare_op=ALU.not_equal, fill=1.0, base=0,
                                    pattern=[[-1, P]], channel_multiplier=1)
            nc.gpsimd.affine_select(out=sel[:, :, :], in_=sel[:, :, :], compare_op=ALU.not_equal, fill=1.0, base=0,
                                    pattern=[[-1, BIASES], [0, P]], channel_multiplier=1).then_inc(s_pool, 1)
            pool.wait_ge(s_pool, 4)
            nc.gpsimd.affine_select(out=sel[:, :, :], in_=sel[:, :, :], compare_op=ALU.not_equal, fill=1.0, base=-LOW0,
                                    pattern=[[-1, BIASES], [0, P]], channel_multiplier=1).then_inc(s_const, 1)
            pool.wait_ge(s_ids, 16)
            nc.gpsimd.tensor_copy(stage_h[:, :], ids[:, 0, :])
            nc.gpsimd.tensor_copy(stage_p[:, :], ids[:, HO0:HO0 + 2 * GT, 0])
            nc.gpsimd.tensor_copy(stage_q[:, :], ids[:, HO0:HO0 + 2 * GT, 1])
            nc.gpsimd.tensor_copy(idf[:, :, :], ids[:, :, :]).then_inc(s_pool, 1)
            pool.wait_ge(s_pool, 5)
            pool.wait_ge(s_hst, 16)
            for c in range(2):
                nc.gpsimd.indirect_dma_start(out=G[:, SLOTS - 2 + c, :], out_offset=None, in_=h_rows,
                                             in_offset=bass.IndirectOffsetOnAxis(ap=stage_h[:, c:c + 1], axis=0)
                                             ).then_inc(s_hg[c], 16)

            def p_rows(slot, table):
                nc.gpsimd.indirect_dma_start(out=G[:, slot, :], out_offset=None, in_=table,
                                             in_offset=bass.IndirectOffsetOnAxis(ap=stage_p[:, slot:slot + 1], axis=0)
                                             ).then_inc(s_gp[slot], 16)

            def q_rows(lap, slot, table):
                pool.wait_ge(s_gp[slot], 16 * (lap + 1))
                pool.sem_inc(s_claim, 1)
                nc.gpsimd.indirect_dma_start(out=G[:, slot, :], out_offset=None, in_=table,
                                             in_offset=bass.IndirectOffsetOnAxis(ap=stage_q[:, slot:slot + 1], axis=0),
                                             compute_op=ALU.add).then_inc(s_gq[slot], 16)

            def pair(i, first, last):
                n0 = SLOTS * i
                lag = SLOTS if first else LAG
                for j in range(SLOTS):
                    if not first:
                        pool.wait_ge(s_used, n0 + j + 1 - SLOTS)
                        pool.sem_inc(s_claim, 1)
                    elif j == 0:
                        pool.wait_ge(s_tab[0], 16)
                        pool.wait_ge(s_hT, 4)
                    elif j == SLOTS - 2:
                        pool.wait_ge(s_hsT, 4)
                    p_rows(j, p_ho)
                    if j == LAG - 1 and not first:
                        for k in range(SLOTS):
                            pool.wait_ge(s_gq[k], 16 * i)
                        pool.sem_inc(s_claim, 1)
                        nc.gpsimd.tensor_copy(stage_q[:, :], ids[:, bass.ds(HO0 + n0, SLOTS), 1]
                                              ).then_inc(s_pool, 1)
                        pool.wait_ge(s_pool, 5 + 2 * i)
                        pool.sem_inc(s_claim, 1)
                    if j >= lag:
                        q_rows(i, j - lag, q_ho)
                if first:
                    pool.wait_ge(s_tab[1], 16)
                for k in range(SLOTS - lag, SLOTS):
                    q_rows(i, k, q_ho)
                if not last:
                    nc.gpsimd.tensor_copy(stage_p[:, :], ids[:, bass.ds(HO0 + n0 + SLOTS, SLOTS), 0]
                                          ).then_inc(s_pool, 1)
                    pool.wait_ge(s_pool, 6 + 2 * i)
                    pool.sem_inc(s_claim, 1)

            pair(0, True, False)
            with pool.Fori(1, PAIRS - 1) as i:
                pair(i, False, False)
            pair(PAIRS - 1, False, True)
            nc.gpsimd.tensor_copy(stage_p[:, 0:OO_TILES], ids[:, 1:HO0, 0]).then_inc(s_pool, 1)
            for k in range(SLOTS):
                pool.wait_ge(s_gq[k], 16 * PAIRS)
            nc.gpsimd.tensor_copy(stage_q[:, 0:OO_TILES], ids[:, 1:HO0, 1]).then_inc(s_pool, 1)
            pool.wait_ge(s_pool, 5 + 2 * (PAIRS - 1) + 2)
            pool.wait_ge(s_tab[2], 16)
            pool.wait_ge(s_tab[3], 16)
            for j in range(OO_TILES):
                pool.wait_ge(s_used, HO_TILES + j + 1 - SLOTS)
                p_rows(j, p_oo)
            for j in range(OO_TILES):
                q_rows(PAIRS, j, q_oo)
            pool.wait_ge(s_used, HO_TILES)
            for i, tile in enumerate(EARLY_TILES):
                nc.gpsimd.tensor_scalar(ohs_end[:, i, :], iota[:, :], idf[:, tile, 0:1], None, ALU.is_equal)
                nc.gpsimd.tensor_scalar(ohd_end[:, i, :], iota[:, :], idf[:, tile, 1:2], None, ALU.is_equal
                                        ).then_inc(s_oh_end, 1)

        @block.scalar
        def _(act):
            act.wait_ge(s_var, NT)
            act.wait_ge(s_const, 1)
            nc.scalar.activation(sd[:, :], mv[:, :, 1], ACT.Sqrt, bias=epst[:, 0:1]).then_inc(s_sd, 1)
            for t in range(NT):
                act.wait_ge(s_nb, 1)
                nc.scalar.activation(h[:, t, :], xs[:, t, :], ACT.Relu, bias=nb[:, t:t + 1],
                                     scale=rs[:, t:t + 1]).then_inc(s_h, 1)
            act.wait_ge(s_h, NT)
            act.dma_start(by_tile(h_rows), h[:, :, :]).then_inc(s_hst, 16)
            def high(q, slot, lap, first=False):
                act.wait_ge(s_w[slot], 16 * (lap + 1))
                if not first:
                    act.wait_ge(s_wused, q - WSLOTS + 1)
                nc.scalar.copy(Wh[:, slot, :], W[:, slot, :]).then_inc(s_hi, 1)

            def highs(q0, q1):
                for q in range(q0, q1):
                    high(q, q % WSLOTS, q // WSLOTS, first=q < WSLOTS)

            def evac_store(u, table, dram, stored, before):
                act.wait_ge(s_wused, KC * (u + 1))
                for b in range(2 * NT):
                    nc.scalar.copy(T[:, table, b // 2, b % 2 * HALF:(b % 2 + 1) * HALF], psG[:, b, :]
                                   ).then_inc(s_evac, 1)
                act.wait_ge(s_evac, before + 2 * NT)
                act.dma_start(by_tile(dram), T[:, table, :, :]).then_inc(stored, 16)

            def hs_high(r):
                act.wait_ge(s_hsT, r + 1)
                nc.scalar.copy(hsh[:, r // 2, 4 * (r % 2):4 * (r % 2) + 4, :],
                               psB[:, r % 2, :].rearrange("p (k e) -> p k e", e=P)).then_inc(s_hsTc, 1)

            for b in range(4):
                highs(b, b + 1)
                act.wait_ge(s_hT, b + 1)
                nc.scalar.copy(hTh[:, 2 * b:2 * b + 2, :], hT_banks[b].rearrange("p (k n) -> p k n", n=N)
                               ).then_inc(s_hTc, 1)
            act.wait_ge(s_ew, 16)
            nc.scalar.copy(ewh[:, :], ew[:, :]).then_inc(s_ewh, 1)
            act.wait_ge(s_small, 48)
            nc.scalar.copy(biases[:, :], brow[:, :]).then_inc(s_bh, 1)
            act.wait_ge(s_const, 1)
            nc.scalar.copy(selr[:, :, :], sel[:, :, :]).then_inc(s_bh, 1)
            highs(4, KC + 3)
            evac_store(0, 0, p_ho, s_tab[0], 0)
            highs(KC + 3, HH_AFTER + 4)
            for r in range(4):
                highs(HH_AFTER + 4 + r, HH_AFTER + 5 + r)
                hs_high(r)
            highs(HH_AFTER + 8, 2 * KC + 3)
            evac_store(1, 1, q_ho, s_tab[1], 4)

            def product(n, r, factors, q):
                act.wait_ge(s_ohs, n + 1)
                for i, val in enumerate(factors):
                    last = nc.scalar.activation(R[:, r, q + i, :], ohs[:, r, :], ACT.Copy, scale=val.bitcast(f32))
                last.then_inc(s_prod, 1)

            def products(g, par, tile0, k0, k1):
                for k in range(k0, k1):
                    col = bass.ds(tile0 + k, 1)
                    product(EARLY + g * GT + k, k % RING,
                            [exh[:, par, k:k + 1], exl[:, par, k:k + 1], ewh[:, col], ewl[:, col]], 0)

            for i in range(EARLY):
                highs(2 * KC + 3 + i, 2 * KC + 4 + i)
                col = slice(EARLY_TILES[i], EARLY_TILES[i] + 1)
                product(i, i % RING, [ewh[:, col], ewl[:, col]], 2)
            highs(2 * KC + 3 + EARLY, 4 * KC + 4)

            def exps(g, par):
                act.wait_ge(s_ed, g + 1)
                nc.scalar.activation(ex[:, par, :], ed[:, par, :], ACT.Exp).then_inc(s_ex, 1)

            def step(g, par, tile0):
                q0, lap = STEP0 + g * STEP, g + STEP0 // STEP
                products(g, par, tile0, 0, 3)
                high(q0 + 2, 2, lap)
                products(g, par, tile0, 3, 4)
                high(q0 + 3, 3, lap)
                products(g, par, tile0, 4, 5)
                exps(g + 1, 1 - par)
                high(q0 + STEP, 0, lap + 1)
                products(g, par, tile0, 5, GT)
                high(q0 + STEP + 1, 1, lap + 1)

            exps(0, 0)
            highs(4 * KC + 4, STEP0 + 2)
            act.wait_ge(s_tab[0], 16)
            evac_store(4, 0, p_oo, s_tab[2], 8)
            step(0, 0, HO0)
            step(1, 1, HO0 + GT)
            act.wait_ge(s_tab[1], 16)
            evac_store(5, 1, q_oo, s_tab[3], 12)
            with act.Fori(1, 1 + VT) as j:
                for r in range(2):
                    step(2 * j + r, r, HO0 + (2 * j + r) * GT)
                act.wait_ge(s_wused, KC * (j + 6))
                for b in range(4):
                    nc.scalar.copy(T[:, bass.ds(j + 1, 1), b // 2, b % 2 * HALF:(b % 2 + 1) * HALF].rearrange("p a d -> p (a d)"),
                                   psG[:, b, :]).then_inc(s_evac, 1)
            for g in range(2 + 2 * VT, 2 * PAIRS - 1):
                step(g, g % 2, HO0 + g * GT)
            q = UNITS * KC - STEP

            def end_product(i):
                act.wait_ge(s_oh_end, i + 1)
                if i % GT == 0:
                    act.wait_ge(s_exs, 2 * PAIRS + i // GT)
                act.wait_ge(s_ohu, END + i - GT + 1 if i >= GT else END - RING + i // 2 + 1)
                for part, val in enumerate((exh, exl)):
                    last = nc.scalar.activation(end_place(i, part), ohs_end[:, i, :], ACT.Copy,
                                                scale=val[:, 1 - i // GT, i % GT:i % GT + 1].bitcast(f32))
                last.then_inc(s_prod, 1)

            for i in range(3):
                end_product(i)
            highs(q + 2, q + 3)
            for i in range(3, GT):
                end_product(i)
            highs(q + 3, q + 4)
            exps(2 * PAIRS, 0)
            for i in range(GT, 2 * GT):
                end_product(i)
            nc.scalar.activation(warm[:, :], epst[:, :], ACT.Sqrt)
            act.wait_ge(s_tab[3], 16)
            act.wait_ge(s_ohu, EARLY + GT * (2 * PAIRS + 1))
            nc.scalar.copy(Wd[:, :, :], psW[:, :, :]).then_inc(s_Wd, 1)
            for j in range(NT):
                act.wait_ge(s_AT, j + 1)
                nc.scalar.copy(AT[:, j, :], psB[:, j, 0:N]).then_inc(s_ATc, 1)
            for n, t in enumerate(TAIL):
                act.wait_ge(s_st2, n + 1)
                nc.scalar.activation(sd[:, t:t + 1], mv[:, t, 1:2], ACT.Sqrt, bias=epst[:, 0:1]).then_inc(s_sd2, 1)
                act.wait_ge(s_nb2, n + 1)
                nc.scalar.activation(h2[:, t, :], x1[:, t, 0:N], ACT.Relu, bias=nb[:, t:t + 1],
                                     scale=rs[:, t:t + 1]).then_inc(s_h2, 1)
                act.wait_ge(s_h2T, n + 1)
                nc.scalar.copy(h2T[:, :, t * P:(t + 1) * P], psB[:, t, 0:N].rearrange("p (j n) -> p j n", n=P)
                               ).then_inc(s_h2Tc, 1)

        @block.vector
        def _(dve):
            steps = [0]

            def chain(ins):
                steps[0] += 1
                ins.then_inc(s_v, 1)
                dve.wait_ge(s_v, steps[0])

            def norm(rows, t, var_sem):
                for b in range(2):
                    chain(nc.vector.bn_stats(st[:, t, b, :], rows[:, t, b * HALF:(b + 1) * HALF]))
                nc.vector.bn_aggr(mv[:, t, :], st[:, t, :, :].rearrange("p b s -> p (b s)")).then_inc(var_sem, 1)

            for t in range(NT):
                dve.wait_ge(s_x[t], 16)
                norm(xs, t, s_var)
            dve.wait_ge(s_sd, 1)
            chain(nc.vector.reciprocal(rs[:, :], sd[:, :]))
            nc.vector.scalar_tensor_tensor(out=nb[:, :], in0=mv[:, :, 0], scalar=-1.0, in1=rs[:, :],
                                           op0=ALU.mult, op1=ALU.mult).then_inc(s_nb, 1)
            def low(q, slot):
                dve.wait_ge(s_hi, q + 1)
                nc.vector.tensor_tensor(Wl[:, slot, :], W[:, slot, :], Wh[:, slot, :].bitcast(f32), ALU.subtract
                                        ).then_inc(s_lo, 1)

            def lows(q0, q1):
                for q in range(q0, q1):
                    low(q, q % WSLOTS)

            def fan_copy(m):
                dve.wait_ge(s_fan, m + 1)
                nc.vector.tensor_copy(dstb[:, fan[m]], fan_bank(m)).then_inc(s_fanc, 1)

            for m in range(FAN_FIRST):
                fan_copy(m)

            def onehots(n, r, tile, first=False):
                if not first:
                    dve.wait_ge(s_ohu, n + 1 - RING)
                nc.vector.tensor_scalar(ohs[:, r, :], iota[:, :], idf[:, bass.ds(tile, 1), 0], None, ALU.is_equal
                                        ).then_inc(s_ohs, 1)
                nc.vector.tensor_scalar(ohd[:, r, :], iota[:, :], idf[:, bass.ds(tile, 1), 1], None, ALU.is_equal
                                        ).then_inc(s_oh, 1)

            def onehot(g, tile0, k):
                onehots(EARLY + g * GT + k, k % RING, tile0 + k)

            for b in range(4):
                lows(b, b + 1)
                dve.wait_ge(s_hTc, b + 1)
                nc.vector.tensor_tensor(hTl[:, 2 * b:2 * b + 2, :], hT_banks[b].rearrange("p (k n) -> p k n", n=N),
                                        hTh[:, 2 * b:2 * b + 2, :].bitcast(f32), ALU.subtract).then_inc(s_hTl, 1)
            dve.wait_ge(s_bh, 2)
            low_rows = slice(LOW0, LOW0 + 32)
            nc.vector.tensor_tensor(biases[low_rows, :], brow[low_rows, :], biases[low_rows, :].bitcast(f32),
                                    ALU.subtract).then_inc(s_bl, 1)
            def hs_low(r):
                dve.wait_ge(s_hsTc, r + 1)
                nc.vector.tensor_tensor(hsl[:, r // 2, 4 * (r % 2):4 * (r % 2) + 4, :],
                                        psB[:, r % 2, :].rearrange("p (k e) -> p k e", e=P),
                                        hsh[:, r // 2, 4 * (r % 2):4 * (r % 2) + 4, :].bitcast(f32), ALU.subtract
                                        ).then_inc(s_hsTl, 1)

            for q in range(4, 2 * KC):
                lows(q, q + 1)
                if q > FAN_FIRST:
                    fan_copy(q - 1)
                if HH_AFTER <= q - 3 < HH_AFTER + 4:
                    hs_low(q - 3 - HH_AFTER)
            for m in (2 * KC - 1, 2 * KC):
                fan_copy(m)
            dve.wait_ge(s_ewh, 1)
            chain(nc.vector.tensor_tensor(ewl[:, :], ew[:, :], ewh[:, :].bitcast(f32), ALU.subtract))
            dve.wait_ge(s_fanc, len(fan))
            dve.wait_ge(s_wa, 16)
            dve.wait_ge(s_small, 48)
            dve.wait_ge(s_const, 1)
            dve.wait_ge(s_pool, 5)

            CH = 13

            def rows(lap, par, k0, k1):
                for k in range(k0, k1):
                    slot = par * GT + k
                    dve.wait_ge(s_gq[slot], 16 * (lap + 1))
                    nc.vector.scalar_tensor_tensor(out=G[:, slot, :], in0=G[:, slot, :], scalar=0.0, in1=wa[:, :],
                                                   op0=ALU.max, op1=ALU.mult, accum_out=lg[:, par, k:k + 1]
                                                   ).then_inc(s_used, 1)

            def logits(g, par, n_used):
                dve.wait_ge(s_used, n_used)
                nc.vector.tensor_scalar(lg[:, par, :], lg[:, par, :], bar[:, 0:1], None, ALU.add).then_inc(s_lg, 1)

            def masks(g, par, base, tile0):
                for c in range(NT):
                    dsts = dstb[:, bass.ds(tile0 * P, GT * P)]
                    nc.vector.tensor_scalar(eqT[:, par, c, :], dsts, pid[:, c:c + 1], None, ALU.is_equal
                                            ).then_inc(s_ind, 1)
                    nc.vector.tensor_scalar(negm[:, c, :], dsts, pid[:, c:c + 1], NEG, ALU.not_equal, ALU.mult
                                            ).then_inc(s_v, 1)

            def post1(g, par, base, tile0=None):
                if tile0 is not None:
                    masks(g, par, base, tile0)
                dve.wait_ge(s_v, base + 2)
                dve.wait_ge(s_bc, g + 1)
                dve.sem_inc(s_rowsok, 1)
                for c in range(NT):
                    nc.vector.tensor_tensor_reduce(
                        out=negm[:, c, :].rearrange("p (a e) -> p a e", a=2), in0=rowsB,
                        in1=negm[:, c, :].rearrange("p (a e) -> p a e", a=2), scale=1.0,
                        scalar=mx[:, 1 - par, c:c + 1], op0=ALU.add, op1=ALU.max,
                        accum_out=mx[:, par, c:c + 1]).then_inc(s_v, 1)
                dve.wait_ge(s_v, base + 4)
                nc.vector.tensor_tensor(ed[:, par, GT:GT + NT], mx[:, 1 - par, :], mx[:, par, :], ALU.subtract
                                        ).then_inc(s_v, 1)
                nc.vector.tensor_copy(msp[:, :, 0], mx[:, par, :]).then_inc(s_v, 1)
                dve.wait_ge(s_v, base + 6)
                nc.vector.tensor_tensor(mres[:, 0, :], mx[:, par, :], msp[:, :, 0], ALU.subtract).then_inc(s_v, 1)
                dve.wait_ge(s_v, base + 7)
                nc.vector.tensor_copy(msp[:, :, 1], mres[:, 0, :]).then_inc(s_v, 1)
                dve.wait_ge(s_v, base + 8)
                nc.vector.tensor_tensor(mres[:, 1, :], mres[:, 0, :], msp[:, :, 1], ALU.subtract).then_inc(s_v, 1)
                dve.wait_ge(s_v, base + 9)
                nc.vector.tensor_copy(msp[:, :, 2], mres[:, 1, :]).then_inc(s_m, 1)

            def post2(g, par, base):
                dve.wait_ge(s_mg, g + 1)
                nc.vector.tensor_reduce(mg[:, :], psM.rearrange("p (t s) -> p t s", s=3), AX.X, ALU.add
                                        ).then_inc(s_v, 1)
                dve.wait_ge(s_v, base + 10)
                nc.vector.tensor_tensor(ed[:, par, 0:GT], lg[:, par, :], mg[:, :], ALU.subtract).then_inc(s_ed, 1)

            def post3(g, par, base):
                dve.wait_ge(s_ex, g + 1)
                nc.vector.tensor_copy(exh[:, par, :], ex[:, par, 0:GT]).then_inc(s_v, 1)
                dve.wait_ge(s_v, base + 11)
                nc.vector.tensor_tensor(exl[:, par, :], ex[:, par, 0:GT], exh[:, par, :].bitcast(f32), ALU.subtract
                                        ).then_inc(s_v, 1)
                dve.wait_ge(s_v, base + 12)
                dve.sem_inc(s_exs, 1)

            def add(g, par, first=False, sums=False):
                dve.wait_ge(s_ohu, EARLY + GT * (g + 1))
                if not first:
                    dve.wait_ge(s_acc, g)
                for c in range(NT):
                    last = nc.vector.scalar_tensor_tensor(out=A[:, c, :], in0=A[:, c, :],
                                                          scalar=ex[:, par, GT + c:GT + c + 1], in1=psA[:, c, :],
                                                          op0=ALU.mult, op1=ALU.add,
                                                          **({"accum_out": den[:, c:c + 1]} if sums else {}))
                last.then_inc(s_acc, 1)

            base0 = steps[0]

            def vbase(g):
                return base0 + g * (CH - 1)

            def step(g, par, row, first=False, second=False):
                tile0 = HO0 + g * GT
                nxt, at = 1 - par, vbase(g + 1)
                lowered = lambda s: low(STEP0 + g * STEP + s, s)

                lowered(0)
                row(0)
                if not first:
                    add(g - 1, nxt, second)
                onehot(g, tile0, 0)
                post1(g + 1, nxt, at, tile0 + GT)
                onehot(g, tile0, 1)
                onehot(g, tile0, 2)
                lowered(1)
                row(1)
                onehot(g, tile0, 3)
                row(2)
                post2(g + 1, nxt, at)
                onehot(g, tile0, 4)
                row(3)
                onehot(g, tile0, 5)
                lowered(2)
                row(4)
                post3(g + 1, nxt, at)
                lowered(3)
                row(5)

            def loop_step(g, j, par, **more):
                step(g, par, lambda k: rows(j + 1, par, k, k + 1), **more)
                logits(g + 2, par, (g + 3) * GT)

            def hh_low(i):
                low(2 * KC + i, i % WSLOTS)
                if i < EARLY:
                    onehots(i, i % RING, EARLY_TILES[i], first=i < RING)

            for i in range(KC):
                hh_low(i)
            for k in range(GT):
                rows(0, 0, k, k + 1)
                for i in range(KC + 2 * k, min(KC + 2 * k + 2, 2 * KC)):
                    hh_low(i)
            logits(0, 0, GT)
            dve.wait_ge(s_wused, KC * 4)
            nc.vector.scalar_tensor_tensor(out=psG[:, 0:2, :].rearrange("p b d -> p (b d)"),
                                           in0=psG[:, 0:2, :].rearrange("p b d -> p (b d)"), scalar=0.0,
                                           in1=wa[:, :], op0=ALU.max, op1=ALU.mult,
                                           accum_out=lg0[:, 0:1]).then_inc(s_hh, 1)
            p_low = lambda k: low(4 * KC + k, k % WSLOTS)
            p_low(0)
            post1(0, 0, vbase(0), HO0)
            for k in range(3):
                p_low(1 + k)
                rows(0, 1, k, k + 1)
            post2(0, 0, vbase(0))
            for k in range(3):
                p_low(4 + k)
                rows(0, 1, 3 + k, 4 + k)
            post3(0, 0, vbase(0))
            p_low(7)
            logits(1, 1, 2 * GT)
            loop_step(0, 0, 0, first=True)
            loop_step(1, 0, 1, second=True)
            with dve.Fori(1, 1 + VT) as j:
                loop_step(2 * j, j, 0)
                loop_step(2 * j + 1, j, 1)
            j = 1 + VT
            loop_step(2 * j, j, 0)
            loop_step(2 * j + 1, j, 1)
            g = 2 * PAIRS - 2

            def last_rows(k):
                if k == 0:
                    nc.vector.tensor_copy(lg[:, 0, 0:1], lg0[:, :]).then_inc(s_used, 1)
                    return
                dve.wait_ge(s_gq[k - 1], 16 * (PAIRS + 1))
                nc.vector.scalar_tensor_tensor(out=G[:, k - 1, :], in0=G[:, k - 1, :], scalar=0.0, in1=wa[:, :],
                                               op0=ALU.max, op1=ALU.mult, accum_out=lg[:, 0, k:k + 1]
                                               ).then_inc(s_used, 1)

            step(g, 0, last_rows)
            g += 1
            last, at = g + 1, vbase(g + 1)
            add(g - 1, 0)
            logits(last, 0, HO_TILES + GT)
            masks(last, 0, at, 0)
            lowered = lambda s: low(STEP0 + g * STEP + s, s)
            post1(last, 0, at)
            post2(last, 0, at)
            post3(last, 0, at)
            add(g, 1)
            lowered(0)
            lowered(1)
            lowered(2)
            lowered(3)
            g = last
            add(g, 0, sums=True)
            steps[0] = vbase(g + 1)
            dve.wait_ge(s_acc, g + 1)
            chain(nc.vector.tensor_scalar(den[:, :], den[:, :], 0.5, None, ALU.max))
            chain(nc.vector.reciprocal(den[:, :], den[:, :]))
            for c in range(NT):
                nc.vector.tensor_scalar(A[:, c, :], A[:, c, :], den[:, c:c + 1], None, ALU.mult).then_inc(s_alpha, 1)
            dve.wait_ge(s_lb, 16)
            dve.wait_ge(s_xlo, 16)
            for n, t in enumerate(TAIL):
                for half in range(2):
                    cols = slice(half * HALF, (half + 1) * HALF)
                    dve.wait_ge(s_up, 2 * n + half + 1)
                    chain(nc.vector.scalar_tensor_tensor(out=x1[:, t, cols], in0=psG[:, 2 * t + half, :], scalar=0.0,
                                                         in1=x1[:, t, cols], op0=ALU.max, op1=ALU.add))
                    chain(nc.vector.bn_stats(st[:, t, half, :], x1[:, t, cols]))
                nc.vector.bn_aggr(mv[:, t, :], st[:, t, :, :].rearrange("p b s -> p (b s)")).then_inc(s_st2, 1)
                dve.wait_ge(s_sd2, n + 1)
                chain(nc.vector.reciprocal(rs[:, t:t + 1], sd[:, t:t + 1]))
                nc.vector.scalar_tensor_tensor(out=nb[:, t:t + 1], in0=mv[:, t, 0:1], scalar=-1.0,
                                               in1=rs[:, t:t + 1], op0=ALU.mult, op1=ALU.mult).then_inc(s_nb2, 1)
            for n, t in enumerate(TAIL):
                nc.vector.tensor_tensor(x1[:, t, N:D], x1[:, t, N:D], brep[:, N:D], ALU.add).then_inc(s_ylo, 1)
                dve.wait_ge(s_h2, n + 1)
                chain(nc.vector.tensor_tensor(x1[:, t, 0:N], x1[:, t, 0:N], brep[:, 0:N], ALU.add))
            for n, t in enumerate(TAIL):
                dve.wait_ge(s_y, n + 1)
                nc.vector.tensor_tensor(x1[:, t, 0:N], x1[:, t, 0:N], (psW, psA)[t][:, 0, :], ALU.add).then_inc(s_o, 1)

        @block.tensor
        def _(pe):
            def fan_out(m):
                nc.tensor.matmul(fan_bank(m), one[:, :], dstb[0:1, fan[m]], start=True, stop=True).then_inc(s_fan, 1)

            def fan_after(q):
                m = q + 2
                if FAN_FIRST <= m < len(fan):
                    if m == FAN_FIRST:
                        pe.wait_ge(s_hTl, 3)
                    else:
                        pe.wait_ge(s_fanc, m)
                    fan_out(m)

            pe.wait_ge(s_one, 1)
            pe.wait_ge(s_dstb, 16)
            for m in range(FAN_FIRST):
                fan_out(m)
            pe.wait_ge(s_const, 1)
            for _ in range(WARM):
                nc.tensor.matmul(hT_banks[3], zero[:, 0:P], zero[:, :], start=True, stop=True)
            for t in range(NT):
                pe.wait_ge(s_h, t + 1)
                for b in range(4):
                    for i in range(2):
                        k = 2 * b + i
                        last = nc.tensor.transpose(hT_banks[b][:, (2 * i + t) * P:(2 * i + t + 1) * P],
                                                   h[:, t, k * P:(k + 1) * P], ident[:, :])
                    if t == NT - 1:
                        last.then_inc(s_hT, 1)

            def free(bank, copied):
                if copied is not None:
                    pe.wait_ge(s_evac, copied + bank + 1)

            def chunk(q, k, tiles, opened=False, last=True, copied=None):
                pe.wait_ge(s_lo, q + 1)
                s = k % WSLOTS
                for high, low, rows, bank in tiles:
                    passes = ((high, Wh), (high, Wl), (low, Wh))
                    for n, (lhs, rhs) in enumerate(passes):
                        for half in range(2):
                            if k == 0 and n == 0:
                                free(bank + half, copied)
                            ins = nc.tensor.matmul(psG[rows, bank + half, :], lhs(k),
                                                   rhs[:, s, half * HALF:(half + 1) * HALF],
                                                   start=not opened and k == 0 and n == 0,
                                                   stop=last and k == KC - 1 and n == 2)
                ins.then_inc(s_wused, 1)

            def bias(row, tiles, copied=None):
                for _, _, rows, bank in tiles:
                    for half in range(2):
                        free(bank + half, copied)
                        nc.tensor.matmul(psG[rows, bank + half, :], selr[:, row, rows],
                                         biases[:, half * HALF:(half + 1) * HALF], start=True, stop=False)

            def node_tile(rows, t):
                cols = slice(t * P + rows.start, t * P + rows.stop)
                return (lambda k: hTh[:, k, cols], lambda k: hTl[:, k, cols], rows, 2 * t)

            nodes = [node_tile(slice(0, P), t) for t in range(NT)]

            pe.wait_ge(s_fanc, FAN_FIRST)
            for k in range(KC):
                if k % 2 == 0:
                    pe.wait_ge(s_hTl, k // 2 + 1)
                chunk(k, k, nodes)
                fan_after(k)
                if k == 3:
                    pe.wait_ge(s_hTl, 4)
                    nc.tensor.matmul(psW[:, :, :].rearrange("p c n -> p (c n)"), zero[:, 0:P], zero[:, :],
                                     start=True, stop=False, skip_group_check=True)
            pe.wait_ge(s_bl, 1)
            pe.wait_ge(s_bh, 2)
            bias(0, nodes, copied=0)
            for k in range(KC):
                chunk(KC + k, k, nodes, opened=True)
                fan_after(KC + k)
                r = KC + k - HH_AFTER
                if 0 <= r < 4:
                    if r % 2 == 0:
                        pe.wait_ge(s_hg[r // 2], 16)
                    if r >= 2:
                        pe.wait_ge(s_hsTl, r - 1)
                    for q in range(4):
                        kk = 4 * (r % 2) + q
                        last = nc.tensor.transpose(psB[:, r % 2, q * P:(q + 1) * P],
                                                   G[:, SLOTS - 2 + r // 2, kk * P:(kk + 1) * P], ident[:, :])
                    last.then_inc(s_hsT, 1)

            def place(n, r, parts):
                pe.wait_ge(s_oh, n + 1)
                pe.wait_ge(s_prod, n + 1)
                for c in range(NT):
                    for q in parts:
                        ins = nc.tensor.matmul((psA if q < 2 else psW)[:, c, :], ohd[:, r, c * P:(c + 1) * P],
                                               R[:, r, q, :], start=False, stop=False, skip_group_check=True)
                ins.then_inc(s_ohu, 1)

            pe.wait_ge(s_hsTl, 4)
            for c in range(2):
                ends = [(lambda k, c=c: hsh[:, c, k, :], lambda k, c=c: hsl[:, c, k, :], slice(0, P), 0)]
                if c == 0:
                    bias(1, ends, copied=4)
                for k in range(KC):
                    chunk((2 + c) * KC + k, k, ends, opened=True, last=c == 1)
                    i = c * KC + k
                    if i < EARLY:
                        place(i, i % RING, (2, 3))

            def spread(g, par):
                pe.wait_ge(s_lg, g + 1)
                for k in range(GT):
                    a, q = divmod(k, GT // 2)
                    last = nc.tensor.matmul(psB[:, a, q * P:(q + 1) * P],
                                            lg[:, par, k:k + 1].broadcast_to((P, P)), ident[:, :],
                                            start=True, stop=True)
                last.then_inc(s_bc, 1)

            def edge_max(g, par):
                pe.wait_ge(s_ind, (g + 1) * 2)
                pe.wait_ge(s_m, g + 1)
                for k in range(GT):
                    for c in range(NT):
                        last = nc.tensor.matmul(psM[:, 3 * k:3 * k + 3], eqT[:, par, c, k * P:(k + 1) * P],
                                                msp[:, c, :], start=c == 0, stop=c == NT - 1)
                last.then_inc(s_mg, 1)

            def clear(g, first=False):
                if not first:
                    pe.wait_ge(s_acc, g)
                nc.tensor.matmul(psA[:, :, :].rearrange("p c n -> p (c n)"), zero[:, 0:P], zero[:, :],
                                 start=True, stop=False, skip_group_check=True)

            def sums(g, k0, k1):
                for k in range(k0, k1):
                    place(EARLY + g * GT + k, k % RING, (0, 1, 2, 3))

            def end_sums(i0, i1):
                for i in range(i0, i1):
                    pe.wait_ge(s_oh_end, i + 1)
                    pe.wait_ge(s_prod, END + i + 1)
                    for c in range(NT):
                        for part in range(2):
                            ins = nc.tensor.matmul(psA[:, c, :], ohd_end[:, i, c * P:(c + 1) * P], end_place(i, part),
                                                   start=False, stop=False, skip_group_check=True)
                    ins.then_inc(s_ohu, 1)

            def step(g, par, q, k0, tiles=nodes, row=None, copied=None, first=False):
                def chunks(n):
                    chunk(q + n, k0 + n, tiles, opened=row is not None, copied=copied if row is None else None)

                if row is not None and k0 == 0:
                    bias(row, tiles, copied)
                chunks(0)
                clear(g, first)
                sums(g, 0, 3)
                edge_max(g + 1, 1 - par)
                chunks(1)
                sums(g, 3, GT)
                chunks(2)
                spread(g + 2, par)
                chunks(3)

            spread(0, 0)
            pe.wait_ge(s_hh, 1)
            for k in range(KC):
                chunk(4 * KC + k, k, nodes, copied=4)
                if k == 3:
                    edge_max(0, 0)
            spread(1, 1)
            copied = lambda j: 8 + 4 * j
            q = lambda g: STEP0 + g * STEP
            step(0, 0, q(0), 0, row=4, copied=copied(0), first=True)
            step(1, 1, q(1), STEP, row=4)
            with pe.Fori(1, 1 + VT) as j:
                step(2 * j, 0, q(2 * j), 0, copied=copied(j))
                step(2 * j + 1, 1, q(2 * j + 1), STEP)
            g = 2 + 2 * VT
            step(g, 0, q(g), 0, row=3, copied=copied(1 + VT))
            step(g + 1, 1, q(g + 1), STEP, row=3)
            heads = [node_tile(slice(0, NH), 0)]
            step(g + 2, 0, q(g + 2), 0, tiles=heads, row=2)
            g += 3
            clear(g)
            end_sums(0, 4)
            edge_max(g + 1, 0)
            end_sums(4, GT)
            clear(g + 1)
            done = GT
            for n, tiles in enumerate((2, 1, 3, 0)):
                end_sums(done, done + tiles)
                chunk(q(g) + n, STEP + n, heads, opened=True)
                done += tiles
            for j in range(NT):
                for c in range(NT):
                    pe.wait_ge(s_alpha, c + 1)
                    last = nc.tensor.transpose(psB[:, j, c * P:(c + 1) * P], A[:, c, j * P:(j + 1) * P], ident[:, :])
                last.then_inc(s_AT, 1)
            pe.wait_ge(s_ATc, NT)
            pe.wait_ge(s_evac, 8 + 4 * 4)
            for t, parts in ((1, ((slice(0, P), 3),)), (0, ((slice(0, NH), 2), (slice(NH, P), 3)))):
                for half in range(2):
                    for rows, v in parts:
                        for j in range(NT):
                            last = nc.tensor.matmul(psG[rows, 2 * t + half, :],
                                                    AT[:, j, t * P + rows.start:t * P + rows.stop],
                                                    T[:, v, j, half * HALF:(half + 1) * HALF],
                                                    start=False, stop=j == NT - 1,
                                                    skip_group_check=True)
                    last.then_inc(s_up, 1)
            pe.wait_ge(s_Wd, 1)
            for n, t in enumerate(TAIL):
                pe.wait_ge(s_h2, n + 1)
                for j in range(NT):
                    last = nc.tensor.transpose(psB[:, t, j * P:(j + 1) * P], h2[:, t, j * P:(j + 1) * P], ident[:, :])
                last.then_inc(s_h2T, 1)
                pe.wait_ge(s_h2Tc, n + 1)
                for j in range(NT):
                    last = nc.tensor.matmul((psW, psA)[t][:, 0, :], h2T[:, j, t * P:(t + 1) * P], Wd[:, j, :],
                                            start=j == 0, stop=j == NT - 1)
                last.then_inc(s_y, 1)


def kernel(**inputs):
    import numpy as np
    import concourse.bacc as bacc
    from concourse.bass_utils import run_bass_kernel_spmd

    a = {k: np.asarray(v) for k, v in inputs.items()}
    D_ = 1024
    top = lambda w: a[f"L0_gnn_W_{w}"][:D_]
    bot = lambda w: a[f"L0_gnn_W_{w}"][D_:]
    cols = lambda v: v.reshape(-1, 128).T
    arrays = {
        "x": a["x"],
        "edge_ids": np.ascontiguousarray(np.stack([cols(a["src"]), cols(a["dst"])], axis=2)),
        "dst_row": np.ascontiguousarray(a["dst"].reshape(1, -1)),
        "edge_w": np.ascontiguousarray(cols(a["edge_weight"])),
        "weights": np.ascontiguousarray(np.concatenate(
            [top("ho"), bot("ho"), top("hh"), bot("hh"), top("oo"), bot("oo"), bot("hn"), bot("on"),
             top("on"), top("hn")])),
        "bias_rows": np.ascontiguousarray(np.stack([a[f"L0_gnn_b_{w}"] for w in ("ho", "hh", "hn", "on", "oo")])),
        "w_a": np.ascontiguousarray(a["L0_gnn_W_a"].reshape(1, -1)),
        "b_a": a["L0_gnn_b_a"].reshape(1, 1),
        "l1_bias": a["L1_gnn_bias"].reshape(1, -1),
    }
    nc = bacc.Bacc("TRN2", target_bir_lowering=False, num_devices=1)
    aps = [nc.dram_tensor(k, v.shape, mybir.dt.from_np(v.dtype), kind="ExternalInput").ap() for k, v in arrays.items()]
    out = nc.dram_tensor("out", a["x"].shape, mybir.dt.float32, kind="ExternalOutput").ap()
    gnn_block(nc, *aps, out)
    return run_bass_kernel_spmd(nc, [arrays], core_ids=[0]).results[0]["out"]
```
